# Optimizing a Trainium2 kernel written in Bass

```python
import numpy as np
import jax
import jax.numpy as jnp

def _softmax(x, axis=-1):
    return jax.nn.softmax(x, axis=axis)

def _gelu(x):
    return jax.nn.gelu(x, approximate=True)

def _silu(x):
    return jax.nn.silu(x)

def _sigmoid(x):
    return jax.nn.sigmoid(x)

def _layernorm(x, axis=-1, eps=1e-05):
    m = jnp.mean(x, axis=axis, keepdims=True)
    v = jnp.var(x, axis=axis, keepdims=True)
    return (x - m) / jnp.sqrt(v + eps)

def _scatter_add(tgt, idx, src, axis=0):
    return tgt.at[idx].add(src)

def _segment_sum(src, seg, n):
    return jax.ops.segment_sum(src, seg, n)
kernel_name = 'mk_rec_standalone_d1_rec_r8_2739f8'

def setup_inputs(seed: int=0):
    np.random.seed(seed)
    _w = jnp.asarray

    def _rec_inputs():
        import jax
        import jax.numpy as jnp
        _rk = jax.random.key(seed)
        r_diag_idx = jax.random.randint(jax.random.fold_in(_rk, 1), (2048, 32, 8), 0, 12500, jnp.int32)
        r_proc_idx = jax.random.randint(jax.random.fold_in(_rk, 2), (2048, 32, 8), 0, 12500, jnp.int32)
        return (r_diag_idx, r_proc_idx)
    r_diag_idx, r_proc_idx = _rec_inputs()

    def _L0_rec_setup():
        import jax, jax.numpy as jnp
        import numpy as np

        def _pool(embedding, idx):
            e = embedding[idx]
            return e.mean(axis=2).sum(axis=1)

        def _lstm(x, W_ih, W_hh, b_ih, b_hh):
            H = W_hh.shape[1]
            gx = x @ W_ih.T + (b_ih + b_hh)

            def step(carry, gx_t):
                h, c = carry
                gates = gx_t + h @ W_hh.T
                i, f, g, o = jnp.split(gates, 4)
                i, f, o = (jax.nn.sigmoid(i), jax.nn.sigmoid(f), jax.nn.sigmoid(o))
                g = jnp.tanh(g)
                c = f * c + i * g
                h = o * jnp.tanh(c)
                return ((h, c), h)
            h0 = jnp.zeros((H,), x.dtype)
            c0 = jnp.zeros((H,), x.dtype)
            _, hs = jax.lax.scan(step, (h0, c0), gx)
            return hs
        key = jax.random.key(seed)
        ks = jax.random.split(key, 12)
        T, A, B = (1024, 32, 8)
        V, D = (12500, 128)
        H1, H2, C = (512, 256, 100)
        s = 0.05
        return {'diag_idx': jax.random.randint(ks[0], (T, A, B), 0, V), 'proc_idx': jax.random.randint(ks[1], (T, A, B), 0, V), 'embedding': jax.random.normal(ks[2], (V, D), jnp.float32) * s, 'W_ih': jax.random.normal(ks[3], (4 * H1, 2 * D), jnp.float32) * s, 'W_hh': jax.random.normal(ks[4], (4 * H1, H1), jnp.float32) * s, 'b_ih': jax.random.normal(ks[5], (4 * H1,), jnp.float32) * s, 'b_hh': jax.random.normal(ks[6], (4 * H1,), jnp.float32) * s, 'W1': jax.random.normal(ks[7], (H2, H1), jnp.float32) * s, 'b1': jax.random.normal(ks[8], (H2,), jnp.float32) * s, 'W_out': jax.random.normal(ks[9], (C, H2), jnp.float32) * s, 'b_out': jax.random.normal(ks[10], (C,), jnp.float32) * s}
    _L0_rec_all = _L0_rec_setup()
    _L0_rec_in = {k: v for k, v in _L0_rec_all.items() if k in ('embedding', 'W_ih', 'W_hh', 'b_ih', 'b_hh', 'W1', 'b1', 'W_out', 'b_out')}
    del _L0_rec_all
    return {'r_diag_idx': r_diag_idx, 'r_proc_idx': r_proc_idx, 'L0_rec_embedding': _L0_rec_in['embedding'], 'L0_rec_W_ih': _L0_rec_in['W_ih'], 'L0_rec_W_hh': _L0_rec_in['W_hh'], 'L0_rec_b_ih': _L0_rec_in['b_ih'], 'L0_rec_b_hh': _L0_rec_in['b_hh'], 'L0_rec_W1': _L0_rec_in['W1'], 'L0_rec_b1': _L0_rec_in['b1'], 'L0_rec_W_out': _L0_rec_in['W_out'], 'L0_rec_b_out': _L0_rec_in['b_out']}

def reference(r_diag_idx, r_proc_idx, L0_rec_embedding, L0_rec_W_ih, L0_rec_W_hh, L0_rec_b_ih, L0_rec_b_hh, L0_rec_W1, L0_rec_b1, L0_rec_W_out, L0_rec_b_out):
    import jax
    import jax.numpy as jnp

    def _L0_rec_ref(diag_idx, proc_idx, embedding, W_ih, W_hh, b_ih, b_hh, W1, b1, W_out, b_out):
        import jax, jax.numpy as jnp
        import numpy as np

        def _pool(embedding, idx):
            e = embedding[idx]
            return e.mean(axis=2).sum(axis=1)

        def _lstm(x, W_ih, W_hh, b_ih, b_hh):
            H = W_hh.shape[1]
            gx = x @ W_ih.T + (b_ih + b_hh)

            def step(carry, gx_t):
                h, c = carry
                gates = gx_t + h @ W_hh.T
                i, f, g, o = jnp.split(gates, 4)
                i, f, o = (jax.nn.sigmoid(i), jax.nn.sigmoid(f), jax.nn.sigmoid(o))
                g = jnp.tanh(g)
                c = f * c + i * g
                h = o * jnp.tanh(c)
                return ((h, c), h)
            h0 = jnp.zeros((H,), x.dtype)
            c0 = jnp.zeros((H,), x.dtype)
            _, hs = jax.lax.scan(step, (h0, c0), gx)
            return hs
        d_vec = _pool(embedding, diag_idx)
        p_vec = _pool(embedding, proc_idx)
        x = jnp.concatenate([d_vec, p_vec], axis=-1)
        hs = _lstm(x, W_ih, W_hh, b_ih, b_hh)
        h1 = jax.nn.relu(hs @ W1.T + b1)
        return h1 @ W_out.T + b_out
    y = _L0_rec_ref(r_diag_idx, r_proc_idx, L0_rec_embedding, L0_rec_W_ih, L0_rec_W_hh, L0_rec_b_ih, L0_rec_b_hh, L0_rec_W1, L0_rec_b1, L0_rec_W_out, L0_rec_b_out)
    return y

_drawn_inputs = setup_inputs


def setup_inputs(seed=0):
    import zlib

    import numpy as np

    out = dict(_drawn_inputs(seed))
    spreads = {}
    factors = {}
    for name, (base, spread) in spreads.items():
        noise = np.random.default_rng([zlib.crc32(name.encode()), seed]).standard_normal(out[name].shape)
        drawn = base * np.exp(spread * noise) if base else spread * noise
        out[name] = jnp.asarray(drawn.astype(out[name].dtype))
    for name, factor in factors.items():
        out[name] = (out[name] * factor).astype(out[name].dtype)
    return out
```

```python
from contextlib import ExitStack

import concourse.bass as bass
from concourse import mybir

ALU = mybir.AluOpType
ACT = mybir.ActivationFunctionType
AX = mybir.AxisListType
F32 = mybir.dt.float32
BF16 = mybir.dt.bfloat16
I32 = mybir.dt.int32
I16 = mybir.dt.int16

P = 128
T = 2048
V, D = 12500, 128
POOLED = 256
MEAN_OVER = 8
HALVES = POOLED // P
ROWS = 2 * T
LO = 128
HI = -(-V // LO)
BLOCK = 128
BLOCKS = ROWS // BLOCK
UNIT = 16
UNITS = BLOCK // UNIT
GROUP = 8
GROUPS = BLOCK // GROUP
CODE = LO + HI
TCHUNKS = 7
THI = HI // TCHUNKS
STAGED = 4

H = 512
G4 = 4 * H
KH = H // P
NJ = H // P
CH = 32
L = T // CH
WARM = 56
TOL = 2.0 ** -19
H2 = 256
C = 100
SEGMENTS = ((0, 0, 256), (1, 256, 128), (2, 384, 128))


def lstm_kernel(nc, raw_idx, table, w_ih, w_hh, b_ih, b_hh, w1, b1, w_out, b_out, out):
    ctx = ExitStack()
    with ctx:
        def sb(name, shape, dt):
            return ctx.enter_context(nc.sbuf_tensor(name, shape, dt))

        def sem(name):
            return ctx.enter_context(nc.semaphore(name))

        tparts = sb("tparts", [P, 3 * HI * D], BF16)
        counts = sb("counts", [P, 2 * HI * BLOCK], BF16)
        codes = sb("codes", [P, 2 * UNIT * HALVES * CODE], BF16)
        xT = sb("xT", [P, ROWS], F32)
        whh = sb("whh", [P, KH * G4], F32)
        raw = sb("raw", [P, 2, BLOCK * HALVES], I32)
        lo2 = sb("lo2", [P, BLOCK * HALVES, 2], I16)
        hi2 = sb("hi2", [P, BLOCK * HALVES, 2], I16)
        ramp = sb("ramp", [P, LO], I16)
        ramp32 = sb("ramp32", [P, LO], I32)
        ident = sb("ident", [P, P], F32)
        shift = sb("shift", [P, P], F32)
        biassel = sb("biassel", [P, CH], BF16)
        ones = sb("ones", [P, P], F32)

        def part(n, hi):
            at = (n * HI + hi) * D
            return tparts[:, at:at + D]

        def cnt(buf):
            return counts[:, buf * HI * BLOCK:(buf + 1) * HI * BLOCK].rearrange("p (h r) -> p h r", r=BLOCK)

        UC = UNIT * HALVES

        def lo_codes(buf):
            at = buf * UC * CODE
            return codes[:, at:at + UC * LO].rearrange("p (c v) -> p c v", v=LO)

        def hi_codes(buf):
            at = buf * UC * CODE + UC * LO
            return codes[:, at:at + UC * HI].rearrange("p (c v) -> p c v", v=HI)

        SW = THI * D
        late_stage = counts[:, HI * BLOCK:HI * BLOCK + 2 * (TCHUNKS - STAGED) * SW].bitcast(F32)

        def stage(k):
            if k < STAGED:
                return whh[:, k * SW:(k + 1) * SW]
            return late_stage[:, (k - STAGED) * SW:(k - STAGED + 1) * SW]

        late = codes[:, :].bitcast(F32)
        wih = late[:, 0:2 * G4].rearrange("p (k n) -> p k n", k=2)
        bias = late[:, 2 * G4:3 * G4]
        bias3 = codes[:, 6 * G4:7 * G4]
        hs = counts[:, 0:2 * KH * T].bitcast(F32).rearrange("p (k c l) -> p k c l", k=KH, c=CH)
        hs_flat = counts[:, 0:2 * KH * T].bitcast(F32).rearrange("p (k t) -> p k t", k=KH)
        rest = tparts[:, :].bitcast(F32)
        taken = [0]

        def carve(n):
            taken[0] += n
            return rest[:, taken[0] - n:taken[0]]

        tanh_g, sig_i, sig_f, sig_o, tanh_c = (carve(P) for _ in range(5))
        ig, fc, c_now, h_now = (carve(P) for _ in range(4))
        hT = [carve(P) for _ in range(2)]
        xs = [carve(2 * CH).rearrange("p (s c) -> p s c", s=2) for _ in range(2)]
        start = carve(2 * P)
        diff = carve(2 * P)
        sq = carve(2 * P)
        agree = carve(2 * P)
        agree_row = carve(1)
        redo = carve(1).bitcast(I32)
        w1_sb = carve(KH * H2).rearrange("p (k n) -> p k n", k=KH)
        wo_sb = carve(2 * C).rearrange("p (k n) -> p k n", k=2)
        b1_sb = carve(2)
        bo_sb = carve(C)
        h1 = [carve(2 * 512).rearrange("p (m n) -> p m n", m=2) for _ in range(2)]
        out_sb = carve(T // P * C).rearrange("p (n c) -> p n c", c=C)
        whh_v = whh[:, :].rearrange("p (k n) -> p k n", k=KH)

        ps = ctx.enter_context(nc.psum_tensor("ps", [P, 8, 512], F32))
        X_BANK = 4
        T_BANK, S_BANK = 6, 7

        raw_in = [sem(f"raw_in{i}") for i in range(2)]
        decoded = sem("decoded")
        codes_ready = sem("codes_ready")
        group_full = sem("group_full")
        group_out = sem("group_out")
        x_full = sem("x_full")
        x_out = sem("x_out")
        table_in = [sem(f"table_in{k}") for k in range(TCHUNKS)]
        tail_zero = sem("tail_zero")
        top_done, mid_done, low_done = sem("top_done"), sem("mid_done"), sem("low_done")
        rest1_done, rest2_done = sem("rest1_done"), sem("rest2_done")
        consts = sem("consts")
        ramp_ready = sem("ramp_ready")
        blank = sem("blank")
        whh_in, wih_in, bias_in, head_in = sem("whh_in"), sem("wih_in"), sem("bias_in"), sem("head_in")
        bias_zero = sem("bias_zero")
        biassel_zero = sem("biassel_zero")
        bias_split = sem("bias_split")
        zero_state = sem("zero_state")
        seam1 = sem("seam1")
        seam1_set = sem("seam1_set")
        seam2 = sem("seam2")
        compare = sem("compare")
        compare_step = sem("compare_step")
        agree_sum = sem("agree_sum")
        redo_set = sem("redo_set")
        seam3 = sem("seam3")
        seam3_set = sem("seam3_set")
        main_stored = sem("main_stored")
        h1_full = sem("h1_full")
        h1_ready = sem("h1_ready")
        y_full = sem("y_full")
        y_out = sem("y_out")
        stored = sem("stored")

        class Run:

            def __init__(self, name, first, steps, keep):
                self.first, self.steps, self.keep = first, steps, keep
                self.xs_ready = sem(name + "_xs_ready")
                self.full = [sem(f"{name}_full{s}") for s in range(3)]
                self.gi = sem(name + "_gi")
                self.f = sem(name + "_f")
                self.tc = sem(name + "_tc")
                self.o = sem(name + "_o")
                self.fc = sem(name + "_fc")
                self.c = sem(name + "_c")
                self.h = sem(name + "_h")
                self.turned = sem(name + "_turned")
                self.hT = sem(name + "_hT")
                self.kept = sem(name + "_kept")

        warm = Run("warm", L - WARM, WARM, False)
        main = Run("main", 0, L, True)
        again = Run("again", 0, L, True)

        block = ctx.enter_context(nc.Block())

        @block.sync
        def _(sp):
            def load_raw(b, buf):
                sp.dma_start(raw[:, buf, :], raw_idx[b]).then_inc(raw_in[buf], 16)

            load_raw(0, 0)
            load_raw(1, 1)
            full = table[0:(HI - 1) * LO, :].rearrange("(h l) d -> l h d", l=LO)
            for k in range(TCHUNKS):
                if k < TCHUNKS - 1:
                    sp.dma_start(stage(k).rearrange("p (h d) -> p h d", d=D),
                                 full[:, k * THI:(k + 1) * THI, :]).then_inc(table_in[k], 16)
                else:
                    sp.dma_start(stage(k)[:, 0:(THI - 1) * D].rearrange("p (h d) -> p h d", d=D),
                                 full[:, k * THI:HI - 1, :]).then_inc(table_in[k], 16)
                    sp.wait_ge(tail_zero, 1)
                    sp.dma_start(stage(k)[0:V - (HI - 1) * LO, (THI - 1) * D:THI * D],
                                 table[(HI - 1) * LO:V, :]).then_inc(table_in[k], 16)
            with sp.Fori(0, BLOCKS // 2 - 1) as i:
                for buf in range(2):
                    sp.wait_ge(decoded, i * 4 + 2 * buf + 2)
                    load_raw(2 * i + buf + 2, buf)
            sp.wait_ge(low_done, TCHUNKS)
            sp.dma_start(whh[:, :], w_hh).then_inc(whh_in, 16)
            sp.wait_ge(group_full, BLOCKS * GROUPS)
            sp.dma_start(late[:, 0:2 * G4], w_ih).then_inc(wih_in, 16)
            sp.wait_ge(bias_zero, 1)
            for q in range(3):
                sp.dma_start(bias[32 * q:32 * q + 1, :], b_ih).then_inc(bias_in, 16)
                sp.dma_start(bias[32 * q + 1:32 * q + 2, :], b_hh).then_inc(bias_in, 16)
            sp.wait_ge(x_full, BLOCKS)
            sp.dma_start(w1_sb, w1.rearrange("p (k n) -> p k n", k=KH)).then_inc(head_in, 16)
            sp.dma_start(wo_sb, w_out.rearrange("p (k n) -> p k n", k=2)).then_inc(head_in, 16)
            sp.dma_start(b1_sb, b1).then_inc(head_in, 16)
            sp.dma_start(bo_sb[0:1, :], b_out).then_inc(head_in, 16)
            out_v = out.rearrange("(n p) c -> p n c", p=P)
            for n in range(4):
                sp.wait_ge(y_out, 4 * n + 4)
                sp.dma_start(out_v[:, 4 * n:4 * n + 4, :], out_sb[:, 4 * n:4 * n + 4, :]).then_inc(stored, 16)
            sp.wait_ge(stored, 16 * 4)

        @block.tensor
        def _(pe):
            def histogram(b, u, first_block=False):
                buf = u % 2
                lo, hi = lo_codes(buf), hi_codes(buf)
                pe.wait_ge(codes_ready, b * UNITS + u + 1)
                for g in range(UNIT // GROUP):
                    if not (first_block and u == 0):
                        pe.wait_ge(group_out, b * GROUPS + 2 * u + g - 1)
                    for r in range(GROUP):
                        at = HI * (r % 4)
                        for half in range(HALVES):
                            col = (g * GROUP + r) * HALVES + half
                            mm = nc.tensor.matmul(ps[:, 2 * g + r // 4, at:at + HI], lo[:, col, :], hi[:, col, :],
                                                  start=(half == 0), stop=(half == HALVES - 1))
                    mm.then_inc(group_full, 1)

            def pool_slice(b, par, u, of):
                if u == 0:
                    pe.wait_ge(group_out, b * GROUPS + GROUPS)
                c = cnt(par)
                for hi in range(HI * u // of, HI * (u + 1) // of):
                    for n in range(3):
                        mm = nc.tensor.matmul(ps[:, X_BANK + par, 0:BLOCK], part(n, hi), c[:, hi, :],
                                              start=(hi == 0 and n == 0), stop=(hi == HI - 1 and n == 2))
                if u == of - 1:
                    mm.then_inc(x_full, 1)

            for u in range(UNITS):
                histogram(0, u, first_block=True)
            pe.wait_ge(low_done, TCHUNKS)
            with pe.Fori(0, BLOCKS // 2 - 1) as i:
                for par in range(2):
                    for u in range(UNITS):
                        histogram(2 * i + par + 1, u)
                        if u == 0 and par == 0:
                            pe.wait_ge(x_out, 2 * i)
                        pool_slice(2 * i + par, par, u, UNITS)
            for u in range(UNITS):
                histogram(BLOCKS - 1, u)
                if u == 0:
                    pe.wait_ge(x_out, BLOCKS - 2)
                pool_slice(BLOCKS - 2, 0, u, UNITS)
            pool_slice(BLOCKS - 1, 1, 0, 1)

            def quad(j):
                return slice(CH * j, CH * j + CH)

            def x_part(r, par, segs):
                for s, c0, n in segs:
                    bank = 3 * par + s
                    for j in range(NJ):
                        nc.tensor.matmul(ps[quad(j), bank, 0:n], biassel[:, :],
                                         bias3[:, j * 512 + c0:j * 512 + c0 + n], start=True, stop=False)
                    for k in range(2):
                        for j in range(NJ):
                            nc.tensor.matmul(ps[quad(j), bank, 0:n], xs[par][:, k, :],
                                             wih[:, k, j * 512 + c0:j * 512 + c0 + n], start=False, stop=False)

            def h_part(r, par):
                for s, c0, n in SEGMENTS:
                    bank = 3 * par + s
                    for k in range(KH):
                        for j in range(NJ):
                            mm = nc.tensor.matmul(ps[quad(j), bank, 0:n], hT[par][:, CH * k:CH * k + CH],
                                                  whh_v[:, k, j * 512 + c0:j * 512 + c0 + n],
                                                  start=False, stop=(k == KH - 1))
                    mm.then_inc(r.full[s], 1)

            def step(r, s, par, more):
                h_part(r, par)
                if more:
                    pe.wait_ge(r.xs_ready, s + 2)
                    x_part(r, 1 - par, SEGMENTS[0:1])
                pe.wait_ge(r.h, s + 1)
                nc.tensor.transpose(ps[:, T_BANK, 0:P], h_now, ident[:, :]).then_inc(r.turned, 1)
                if more:
                    x_part(r, 1 - par, SEGMENTS[1:])
                    pe.wait_ge(r.hT, s + 1)

            def run(r, base, begin):
                pe.wait_ge(r.xs_ready, base + 1)
                x_part(r, 0, SEGMENTS)
                begin()
                with pe.Fori(0, r.steps // 2 - 1) as i:
                    for par in range(2):
                        step(r, base + 2 * i + par, par, True)
                for par in range(2):
                    step(r, base + r.steps - 2 + par, par, par == 0)

            def seam(done):
                nc.tensor.matmul(ps[:, S_BANK, 0:P], shift[:, :], c_now, start=True, stop=True)
                nc.tensor.matmul(ps[:, S_BANK, P:2 * P], h_now, shift[:, :], start=True, stop=True).then_inc(done, 1)

            def begin_warm():
                pe.wait_ge(zero_state, 2)
                pe.wait_ge(whh_in, 16)

            pe.wait_ge(wih_in, 16)
            pe.wait_ge(bias_split, 5)
            pe.wait_ge(consts, 4)
            run(warm, 0, begin_warm)
            seam(seam1)
            run(main, 0, lambda: pe.wait_ge(seam1_set, 1))
            seam(seam2)
            pe.wait_ge(compare, 1)
            nc.tensor.matmul(ps[0:1, T_BANK, 0:1], agree_row, ones[:, 0:1], start=True, stop=True)\
                .then_inc(agree_sum, 1)
            pe.wait_ge(redo_set, 1)
            flag = pe.value_load(redo[0:1, 0:1], min_val=0, max_val=1)
            with pe.If(flag > 0):
                with pe.Fori(0, CH - 1) as n:
                    seam(seam3)
                    pe.wait_ge(seam3_set, n + 1)
                    run(again, n * L, lambda: None)
                pe.wait_ge(again.kept, (CH - 1) * L + 2)
            pe.wait_ge(main.kept, L + 2)
            pe.wait_ge(head_in, 64)

            for n in range(4):
                for m in range(2):
                    q = 2 * n + m
                    if q >= 4:
                        pe.wait_ge(h1_ready, q - 3)
                    for k in range(KH):
                        mm = nc.tensor.matmul(ps[:, q % 4, :], w1_sb[:, k, m * P:(m + 1) * P],
                                              hs_flat[:, k, 512 * n:512 * n + 512],
                                              start=(k == 0), stop=(k == KH - 1))
                    mm.then_inc(h1_full, 1)
                pe.wait_ge(h1_ready, 2 * n + 2)
                for t in range(4):
                    y = 4 * n + t
                    if y >= 2:
                        pe.wait_ge(y_out, y - 1)
                    o = ps[:, 4 + y % 2, 0:C]
                    nc.tensor.matmul(o, ones[0:1, :], bo_sb[0:1, :], start=True, stop=False)
                    for m in range(2):
                        mm = nc.tensor.matmul(o, h1[n % 2][:, m, P * t:P * t + P], wo_sb[:, m, :],
                                              start=False, stop=(m == 1))
                    mm.then_inc(y_full, 1)

        @block.scalar
        def _(act):
            def tpart(n, k):
                at = (n * HI + k * THI) * D
                return tparts[:, at:at + THI * D]

            def split(step):
                if step < TCHUNKS:
                    act.wait_ge(table_in[step], 32 if step == TCHUNKS - 1 else 16)
                    nc.scalar.activation(tpart(0, step), stage(step), ACT.Copy).then_inc(top_done, 1)
                if 0 <= step - 1 < TCHUNKS:
                    act.wait_ge(rest1_done, step)
                    nc.scalar.activation(tpart(1, step - 1), stage(step - 1), ACT.Copy).then_inc(mid_done, 1)
                if 0 <= step - 2 < TCHUNKS:
                    act.wait_ge(rest2_done, step - 1)
                    nc.scalar.activation(tpart(2, step - 2), stage(step - 2), ACT.Copy).then_inc(low_done, 1)

            def counts_out(b, par, g):
                act.wait_ge(group_full, b * GROUPS + g + 1)
                at = ps[:, 2 * (g % 2):2 * (g % 2) + 2, 0:4 * HI].rearrange("p b (r h) -> p h b r", h=HI)
                nc.scalar.activation(cnt(par)[:, :, g * GROUP:(g + 1) * GROUP].rearrange("p h (b r) -> p h b r", b=2),
                                     at, ACT.Copy).then_inc(group_out, 1)

            def x_rows_out(b, par):
                act.wait_ge(x_full, b + 1)
                nc.scalar.activation(xT[:, bass.ds(b * BLOCK, BLOCK)], ps[:, X_BANK + par, 0:BLOCK], ACT.Copy,
                                     scale=1.0 / MEAN_OVER).then_inc(x_out, 1)

            for g in range(GROUPS):
                if g % 2 == 0:
                    split(g // 2)
                counts_out(0, 0, g)
            split(UNITS)
            for g in range(GROUPS):
                counts_out(1, 1, g)
            with act.Fori(0, BLOCKS // 2 - 1) as i:
                for par in range(2):
                    x_rows_out(2 * i + par, par)
                    for g in range(GROUPS):
                        counts_out(2 * i + par + 2, par, g)
            for par in range(2):
                x_rows_out(BLOCKS - 2 + par, par)

            def step(r, s, par):
                b = 3 * par
                act.wait_ge(r.full[0], s + 1)
                nc.scalar.activation(tanh_g, ps[:, b, 0:P], ACT.Tanh)
                nc.scalar.activation(sig_i, ps[:, b, P:2 * P], ACT.Sigmoid).then_inc(r.gi, 1)
                act.wait_ge(r.full[1], s + 1)
                nc.scalar.activation(sig_f, ps[:, b + 1, 0:P], ACT.Sigmoid).then_inc(r.f, 1)
                act.wait_ge(r.full[2], s + 1)
                nc.scalar.activation(sig_o, ps[:, b + 2, 0:P], ACT.Sigmoid).then_inc(r.o, 1)
                act.wait_ge(r.c, s + 1)
                nc.scalar.activation(tanh_c, c_now, ACT.Tanh).then_inc(r.tc, 1)

            def run(r, base):
                with act.Fori(0, r.steps // 2) as i:
                    for par in range(2):
                        step(r, base + 2 * i + par, par)

            run(warm, 0)
            run(main, 0)
            act.wait_ge(redo_set, 1)
            flag = act.value_load(redo[0:1, 0:1], min_val=0, max_val=1)
            with act.If(flag > 0):
                with act.Fori(0, CH - 1) as n:
                    run(again, n * L)
            act.wait_ge(head_in, 64)
            for n in range(4):
                if n >= 2:
                    act.wait_ge(y_full, 4 * (n - 1))
                for m in range(2):
                    q = 2 * n + m
                    act.wait_ge(h1_full, q + 1)
                    nc.scalar.activation(h1[n % 2][:, m, :], ps[:, q % 4, :], ACT.Relu,
                                         bias=b1_sb[:, m:m + 1]).then_inc(h1_ready, 1)

        @block.vector
        def _(dve):
            nc.vector.memset(biassel[:, :], 0.0).then_inc(biassel_zero, 1)
            dve.wait_ge(biassel_zero, 1)
            for q in range(3):
                last = nc.vector.memset(biassel[32 * q:32 * q + 2, :], 1.0)
            last.then_inc(consts, 1)
            dve.wait_ge(ramp_ready, 1)
            nc.vector.tensor_copy(ramp[:, :], ramp32[:, :]).then_inc(ramp_ready, 1)
            dve.wait_ge(ramp_ready, 2)

            def decode(b, buf):
                dve.wait_ge(raw_in[buf], 16 * b + 16)
                low16 = raw[:, buf, :].bitcast(I16).rearrange("p (c e) -> p c e", e=2)[:, :, 0:1]\
                    .to_broadcast([P, BLOCK * HALVES, 2])
                nc.vector.tensor_scalar(lo2[:, :, :], low16, LO - 1, None, ALU.bitwise_and).then_inc(decoded, 1)
                nc.vector.tensor_scalar(hi2[:, :, :], low16, 7, None, ALU.logical_shift_right).then_inc(decoded, 1)

            def one_hot(codes_v, n, pairs, u):
                c = pairs[:, UC * u:UC * u + UC, :].unsqueeze(2).to_broadcast([P, UC, n // 2, 2])
                r = ramp[:, 0:n].rearrange("p (v e) -> p v e", e=2).unsqueeze(1).to_broadcast([P, UC, n // 2, 2])
                return nc.vector.tensor_tensor(codes_v.rearrange("p c (v e) -> p c v e", e=2), c, r, ALU.is_equal)

            def code_block(pair, b, buf, first=False):
                if not first:
                    dve.wait_ge(codes_ready, b * UNITS)
                decode(pair, buf)
                dve.wait_ge(decoded, 2 * b + 2)
                for u in range(UNITS):
                    if not (first and u < 2):
                        dve.wait_ge(group_full, b * GROUPS + 2 * (u - 1))
                    one_hot(lo_codes(u % 2), LO, lo2, u)
                    one_hot(hi_codes(u % 2), HI, hi2, u).then_inc(codes_ready, 1)

            code_block(0, 0, 0, first=True)
            code_block(0, 1, 1)
            with dve.Fori(1, BLOCKS // 2) as i:
                for buf in range(2):
                    code_block(i, 2 * i + buf, buf)

            dve.wait_ge(group_full, BLOCKS * GROUPS)
            nc.vector.memset(bias3, 0.0)
            nc.vector.memset(bias, 0.0).then_inc(bias_zero, 1)
            dve.wait_ge(bias_in, 16 * 6)
            dve.wait_ge(bias_zero, 1)
            done = 0
            for part_n in range(3):
                for q in range(part_n, 3):
                    rows = slice(32 * q, 32 * q + 32)
                    last = nc.vector.tensor_copy(bias3[rows, :], bias[rows, :])
                last.then_inc(bias_split, 1)
                done += 1
                if part_n < 2:
                    dve.wait_ge(bias_split, done)
                    for q in range(part_n + 1, 3):
                        rows = slice(32 * q, 32 * q + 32)
                        last = nc.vector.tensor_tensor(bias[rows, :], bias[rows, :], bias3[rows, :], ALU.subtract)
                    last.then_inc(bias_split, 1)
                    done += 1
                    dve.wait_ge(bias_split, done)

            dve.wait_ge(x_full, BLOCKS)
            nc.vector.memset(hT[0], 0.0).then_inc(zero_state, 1)
            nc.vector.memset(c_now, 0.0).then_inc(zero_state, 1)
            dve.wait_ge(zero_state, 2)

            def step(r, s, par):
                dve.wait_ge(r.gi, s + 1)
                nc.vector.tensor_tensor(ig, sig_i, tanh_g, ALU.mult)
                dve.wait_ge(r.f, s + 1)
                nc.vector.tensor_tensor(fc, sig_f, c_now, ALU.mult).then_inc(r.fc, 1)
                dve.wait_ge(r.fc, s + 1)
                nc.vector.tensor_tensor(c_now, fc, ig, ALU.add).then_inc(r.c, 1)
                dve.wait_ge(r.o, s + 1)
                dve.wait_ge(r.tc, s + 1)
                nc.vector.tensor_tensor(h_now, sig_o, tanh_c, ALU.mult).then_inc(r.h, 1)
                if r.keep:
                    dve.wait_ge(r.kept, s + 1)
                dve.wait_ge(r.turned, s + 1)
                nc.vector.tensor_copy(hT[1 - par], ps[:, T_BANK, 0:P]).then_inc(r.hT, 1)

            def run(r, base):
                with dve.Fori(0, r.steps // 2) as i:
                    for par in range(2):
                        step(r, base + 2 * i + par, par)

            run(warm, 0)
            dve.wait_ge(seam1, 1)
            dve.wait_ge(warm.hT, WARM)
            nc.vector.tensor_copy(c_now, ps[:, S_BANK, 0:P])
            nc.vector.tensor_copy(hT[0], ps[:, S_BANK, P:2 * P])
            nc.vector.tensor_copy(start, ps[:, S_BANK, 0:2 * P]).then_inc(seam1_set, 1)
            dve.wait_ge(seam1_set, 1)
            run(main, 0)

            dve.wait_ge(seam2, 1)
            nc.vector.tensor_tensor(diff, ps[:, S_BANK, 0:2 * P], start, ALU.subtract).then_inc(compare_step, 1)
            dve.wait_ge(compare_step, 1)
            nc.vector.tensor_tensor(sq, diff, diff, ALU.mult).then_inc(compare_step, 1)
            dve.wait_ge(compare_step, 2)
            nc.vector.tensor_scalar(agree, sq, TOL * TOL, None, ALU.is_le).then_inc(compare_step, 1)
            dve.wait_ge(compare_step, 3)
            nc.vector.tensor_reduce(agree_row, agree, AX.X, ALU.add).then_inc(compare, 1)
            dve.wait_ge(agree_sum, 1)
            nc.vector.tensor_scalar(redo[0:1, :], ps[0:1, T_BANK, 0:1], float(2 * P * P), None, ALU.is_lt)\
                .then_inc(redo_set, 1)
            dve.wait_ge(redo_set, 1)
            flag = dve.value_load(redo[0:1, 0:1], min_val=0, max_val=1)
            with dve.If(flag > 0):
                with dve.Fori(0, CH - 1) as n:
                    dve.wait_ge(seam3, n + 1)
                    nc.vector.tensor_copy(c_now, ps[:, S_BANK, 0:P])
                    dve.wait_ge(main.hT, L)
                    dve.wait_ge(again.hT, n * L)
                    dve.wait_ge(main.kept, L + 2)
                    dve.wait_ge(again.kept, n * L + 2)
                    nc.vector.tensor_copy(hT[0], ps[:, S_BANK, P:2 * P]).then_inc(seam3_set, 1)
                    run(again, n * L)

            for y in range(T // P):
                dve.wait_ge(y_full, y + 1)
                nc.vector.tensor_copy(out_sb[:, y, :], ps[:, 4 + y % 2, 0:C]).then_inc(y_out, 1)

        @block.gpsimd
        def _(pool):
            nc.gpsimd.iota(ramp32[:, :], pattern=[[1, LO]], base=0, channel_multiplier=0).then_inc(ramp_ready, 1)
            nc.gpsimd.memset(stage(TCHUNKS - 1)[:, (THI - 1) * D:THI * D], 0.0).then_inc(tail_zero, 1)
            nc.gpsimd.memset(ident[:, :], 0.0).then_inc(blank, 1)
            nc.gpsimd.memset(shift[:, :], 0.0).then_inc(blank, 1)
            nc.gpsimd.memset(ones[:, :], 1.0).then_inc(consts, 1)
            pool.wait_ge(blank, 2)
            nc.gpsimd.affine_select(out=ident[:, :], in_=ident[:, :], compare_op=ALU.not_equal, fill=1.0,
                                    base=0, pattern=[[-1, P]], channel_multiplier=1).then_inc(consts, 1)
            nc.gpsimd.affine_select(out=shift[:, :], in_=shift[:, :], compare_op=ALU.not_equal, fill=1.0,
                                    base=1, pattern=[[-1, P]], channel_multiplier=1).then_inc(blank, 1)
            pool.wait_ge(blank, 3)
            nc.gpsimd.memset(shift[:, :].rearrange("p (j c) -> p j c", c=CH)[:, :, 0:1], 0.0).then_inc(consts, 1)

            def rest(n, k, wait, done):
                pool.wait_ge(wait, k + 1)
                at = (n * HI + k * THI) * D
                nc.gpsimd.tensor_tensor(stage(k), stage(k), tparts[:, at:at + THI * D], ALU.subtract).then_inc(done, 1)

            for step in range(TCHUNKS + 1):
                if step < TCHUNKS:
                    rest(0, step, top_done, rest1_done)
                if step >= 1:
                    rest(1, step - 1, mid_done, rest2_done)

            x_v = xT[:, :].rearrange("p (s c l) -> p s c l", s=2, c=CH)

            def fetch(r, l, par):
                nc.gpsimd.tensor_copy(xs[par].unsqueeze(3), x_v[:, :, :, bass.ds(l + r.first, 1)])\
                    .then_inc(r.xs_ready, 1)

            def keep(r, l, par):
                if r.keep:
                    nc.gpsimd.tensor_copy(hs[:, :, :, bass.ds(l, 1)],
                                          hT[1 - par].rearrange("p (k c) -> p k c", k=KH).unsqueeze(3))\
                        .then_inc(r.kept, 1)

            def keep_last(r, l, par):
                if r.keep:
                    h = hT[1 - par].rearrange("p (k c) -> p k c", k=KH).unsqueeze(3)
                    one = ones[:, :].rearrange("p (k c) -> p k c", k=KH).unsqueeze(3)
                    nc.gpsimd.tensor_tensor(hs[:, :, :, l:l + 1], h, one, ALU.mult).then_inc(r.kept, 1)

            def run(r, base):
                for par in range(2):
                    fetch(r, par, par)
                with pool.Fori(0, r.steps // 2 - 1) as i:
                    for par in range(2):
                        pool.wait_ge(r.hT, base + 2 * i + par + 1)
                        fetch(r, 2 * i + par + 2, par)
                        keep(r, 2 * i + par, par)
                for par in range(2):
                    pool.wait_ge(r.hT, base + r.steps - 1 + par)
                    keep_last(r, r.steps - 2 + par, par)

            pool.wait_ge(x_out, BLOCKS)
            pool.sem_inc(main.kept, 2)
            run(warm, 0)
            run(main, 0)
            pool.wait_ge(redo_set, 1)
            flag = pool.value_load(redo[0:1, 0:1], min_val=0, max_val=1)
            with pool.If(flag > 0):
                pool.sem_inc(again.kept, 2)
                with pool.Fori(0, CH - 1) as n:
                    run(again, n * L)


def kernel(r_diag_idx, r_proc_idx, L0_rec_embedding, L0_rec_W_ih, L0_rec_W_hh, L0_rec_b_ih, L0_rec_b_hh,
           L0_rec_W1, L0_rec_b1, L0_rec_W_out, L0_rec_b_out):
    import numpy as np
    import concourse.bacc as bacc
    from concourse.bass_utils import run_bass_kernel_spmd

    def a(x):
        return np.asarray(x)

    idx = np.stack([a(r_diag_idx), a(r_proc_idx)]).reshape(BLOCKS, BLOCK, HALVES, P).transpose(0, 3, 1, 2)
    order = [2, 0, 1, 3]

    def gates(w):
        return w.reshape(4, NJ, P, -1)[order].transpose(1, 0, 2, 3).reshape(G4, -1)

    def tall(w):
        n = w.shape[0]
        return w.reshape(n, -1, P).transpose(2, 1, 0).reshape(P, -1)

    arrays = {
        "raw_idx": idx.reshape(BLOCKS, P, BLOCK * HALVES),
        "table": a(L0_rec_embedding),
        "w_ih": tall(gates(a(L0_rec_W_ih))),
        "w_hh": tall(gates(a(L0_rec_W_hh))),
        "b_ih": gates(a(L0_rec_b_ih)).reshape(1, G4),
        "b_hh": gates(a(L0_rec_b_hh)).reshape(1, G4),
        "w1": tall(a(L0_rec_W1)),
        "b1": a(L0_rec_b1).reshape(2, P).T,
        "w_out": tall(a(L0_rec_W_out)),
        "b_out": a(L0_rec_b_out).reshape(1, C),
    }
    arrays = {name: np.ascontiguousarray(x) for name, x in arrays.items()}
    nc = bacc.Bacc("TRN2", target_bir_lowering=False, num_devices=1)
    args = [nc.dram_tensor(name, x.shape, mybir.dt.from_np(x.dtype), kind="ExternalInput").ap()
            for name, x in arrays.items()]
    out = nc.dram_tensor("out", (T, C), F32, kind="ExternalOutput").ap()
    lstm_kernel(nc, *args, out)
    got = run_bass_kernel_spmd(nc, [arrays], core_ids=[0])
    return got.results[0]["out"]
```

```python
from contextlib import ExitStack

import concourse.bass as bass
from concourse import mybir

ALU = mybir.AluOpType
ACT = mybir.ActivationFunctionType
AX = mybir.AxisListType
F32 = mybir.dt.float32
BF16 = mybir.dt.bfloat16
I32 = mybir.dt.int32
I16 = mybir.dt.int16

P = 128
T = 2048
V, D = 12500, 128
POOLED = 256
MEAN_OVER = 8
HALVES = POOLED // P
ROWS = 2 * T
LO = 128
HI = -(-V // LO)
BLOCK = 128
BLOCKS = ROWS // BLOCK
UNIT = 8
UNITS = BLOCK // UNIT
CODE = LO + HI
TCHUNKS = 7
THI = HI // TCHUNKS
STAGED = 4

H = 512
G4 = 4 * H
KH = H // P
NJ = H // P
CH = 32
L = T // CH
WARM = 52
TOL = 2.0 ** -19
H2 = 256
C = 100
FIRST = L - WARM
WARM_BLOCKS = WARM // 2
HALF = UNITS // 2
GIF, OUTG = (0, 0, 384), (1, 384, 128)


def lstm_kernel(nc, raw_idx, table, w_ih, w_hh, b_ih, b_hh, w1, b1, w_out, b_out, out):
    ctx = ExitStack()
    with ctx:
        def sb(name, shape, dt):
            return ctx.enter_context(nc.sbuf_tensor(name, shape, dt))

        def sem(name):
            return ctx.enter_context(nc.semaphore(name))

        tparts = sb("tparts", [P, 3 * HI * D], BF16)
        counts = sb("counts", [P, 2 * HI * BLOCK], BF16)
        codes = sb("codes", [P, 2 * UNIT * HALVES * CODE], BF16)
        whh = sb("whh", [P, KH * G4], F32)
        wih_sb = sb("wih", [P, 2 * G4], F32)
        bias3 = sb("bias3", [P, G4], BF16)
        raw = sb("raw", [P, 2, BLOCK * HALVES], I32)
        lo2 = sb("lo2", [P, BLOCK * HALVES, 2], I16)
        hi2 = sb("hi2", [P, BLOCK * HALVES, 2], I16)
        ramp = sb("ramp", [P, LO], I16)
        ramp32 = counts[:, 0:2 * LO].bitcast(I32)
        ident = sb("ident", [P, P], F32)
        shift = sb("shift", [P, P], F32)
        biassel = sb("biassel", [P, CH], BF16)
        ones = sb("ones", [P, P], F32)
        xparts = sb("xparts", [P, 2, 3 * D], F32)
        xT_new = sb("xT_new", [P, 2, BLOCK], F32)
        xT_old = sb("xT_old", [P, 2, BLOCK], F32)

        tparts_v = tparts[:, :].rearrange("p (h n d) -> p h n d", n=3, d=D)

        def parts(hi):
            return tparts[:, hi * 3 * D:(hi + 1) * 3 * D]

        def tpart(n, k):
            return tparts_v[:, k * THI:(k + 1) * THI, n, :]

        def cnt(buf):
            return counts[:, buf * HI * BLOCK:(buf + 1) * HI * BLOCK].rearrange("p (h r) -> p h r", r=BLOCK)

        UC = UNIT * HALVES

        def lo_codes(buf):
            at = buf * UC * CODE
            return codes[:, at:at + UC * LO].rearrange("p (c v) -> p c v", v=LO)

        def hi_codes(buf):
            at = buf * UC * CODE + UC * LO
            return codes[:, at:at + UC * HI].rearrange("p (c v) -> p c v", v=HI)

        SW = THI * D
        late_stage = counts[:, HI * BLOCK:HI * BLOCK + 2 * (TCHUNKS - STAGED) * SW].bitcast(F32)

        def stage(k):
            if k < STAGED:
                return whh[:, k * SW:(k + 1) * SW]
            return late_stage[:, (k - STAGED) * SW:(k - STAGED + 1) * SW]

        def stage_v(k):
            return stage(k).rearrange("p (h d) -> p h d", d=D)

        bias = wih_sb[:, 0:G4]
        wih = wih_sb[:, :].rearrange("p (k n) -> p k n", k=2)
        hs = counts[:, 0:2 * KH * T].bitcast(F32).rearrange("p (k c l) -> p k c l", k=KH, c=CH)
        hs_flat = counts[:, 0:2 * KH * T].bitcast(F32).rearrange("p (k t) -> p k t", k=KH)
        rest = tparts[:, :].bitcast(F32)
        taken = [0]

        def carve(n):
            taken[0] += n
            return rest[:, taken[0] - n:taken[0]]

        def tile(name, n):
            return sb(name, [P, n], F32)[:, :]

        gc = tile("gc", 2 * P)
        sig_if = tile("sig_if", 2 * P)
        products = tile("products", 2 * P)
        tanh_g, c_now = gc[:, 0:P], gc[:, P:2 * P]
        sig_o, tanh_c, h_now = (tile(name, P) for name in ("sig_o", "tanh_c", "h_now"))
        hT = [tile(f"hT{i}", P) for i in range(2)]
        start = tile("start", 2 * P)
        diff = carve(2 * P)
        sq = carve(2 * P)
        agree = carve(2 * P)
        agree_row = carve(1)
        redo = carve(1).bitcast(I32)
        w1_sb = carve(KH * H2).rearrange("p (k n) -> p k n", k=KH)
        wo_sb = carve(2 * C).rearrange("p (k n) -> p k n", k=2)
        b1_sb = carve(2)
        bo_sb = carve(C)
        h1 = [carve(2 * 512).rearrange("p (m n) -> p m n", m=2) for _ in range(2)]
        out_sb = carve(T // P * C).rearrange("p (n c) -> p n c", c=C)
        whh_v = whh[:, :].rearrange("p (k n) -> p k n", k=KH)

        ps = ctx.enter_context(nc.psum_tensor("ps", [P, 8, 512], F32))
        X_BANK = 4
        T_BANK = 6
        S_BANK = 7

        def xT_ps(par):
            return ps[:, T_BANK, par * BLOCK:(par + 1) * BLOCK]

        hT_ps = ps[:, T_BANK, 2 * P:3 * P]

        def early(par):
            return lambda rows, s: ps[rows, S_BANK, 0:3 * P] if s == 0 else ps[rows, X_BANK + par, 3 * P:4 * P]

        def later(par):
            return lambda rows, s: ps[rows, 2 * par + s, 0:(3 * P if s == 0 else P)]

        EVERY = slice(0, P)

        raw_in = [sem(f"raw_in{i}") for i in range(2)]
        decoded = sem("decoded")
        codes_ready = sem("codes_ready")
        counts_full = sem("counts_full")
        counts_out = sem("counts_out")
        x_full = sem("x_full")
        x_out = sem("x_out")
        x_half = sem("x_half")
        x_summed = sem("x_summed")
        xT_full = sem("xT_full")
        xT_out = sem("xT_out")
        xT_kept = [sem(f"xT_kept{i}") for i in range(2)]
        table_in = [sem(f"table_in{k}") for k in range(TCHUNKS)]
        tail_zero = sem("tail_zero")
        top_done, mid_done, low_done = sem("top_done"), sem("mid_done"), sem("low_done")
        rest1_done, rest2_done = sem("rest1_done"), sem("rest2_done")
        ones_set, ident_set, shift_set, biassel_set = (sem(x) for x in ("ones_set", "ident_set", "shift_set",
                                                                         "biassel_set"))
        ramp_ready = sem("ramp_ready")
        blank = sem("blank")
        whh_in, wih_in, bias_in, head_in = sem("whh_in"), sem("wih_in"), sem("bias_in"), sem("head_in")
        bias_zero = sem("bias_zero")
        biassel_zero = sem("biassel_zero")
        bias_split, bias_rest, bias3_zero = sem("bias_split"), sem("bias_rest"), sem("bias3_zero")
        warm_c_zero = sem("warm_c_zero")
        seam1 = sem("seam1")
        seam1_set = sem("seam1_set")
        seam2 = sem("seam2")
        compare = sem("compare")
        compare_step = sem("compare_step")
        agree_sum = sem("agree_sum")
        redo_set = sem("redo_set")
        restarted = sem("restarted")
        h1_full = sem("h1_full")
        h1_ready = sem("h1_ready")
        y_full = sem("y_full")
        y_out = sem("y_out")
        stored = sem("stored")

        x_dram = nc.dram_tensor("x_dram", (BLOCKS, P, BLOCK), F32, kind="Internal").ap()

        class Run:

            def __init__(self, name, keep):
                self.keep = keep
                self.x_in = [sem(f"{name}_x_in{i}") for i in range(2)]
                self.full = [sem(f"{name}_full{s}") for s in range(2)]
                self.gif = sem(name + "_gif")
                self.tc = sem(name + "_tc")
                self.o = sem(name + "_o")
                self.terms = sem(name + "_terms")
                self.c = sem(name + "_c")
                self.h = sem(name + "_h")
                self.turned = sem(name + "_turned")
                self.hT = sem(name + "_hT")
                self.kept = sem(name + "_kept")

        warm = Run("warm", False)
        main = Run("main", True)
        again = Run("again", True)

        def redo_needed(eng, n):
            eng.wait_ge(redo_set, n + 1)
            return eng.If(eng.value_load(redo[0:1, 0:1], min_val=0, max_val=1) > 0)

        block = ctx.enter_context(nc.Block())

        @block.sync
        def _(sp):
            def load_raw(b, buf):
                sp.dma_start(raw[:, buf, :], raw_idx[b]).then_inc(raw_in[buf], 16)

            load_raw(0, 0)
            load_raw(1, 1)
            full = table[0:(HI - 1) * LO, :].rearrange("(h l) d -> l h d", l=LO)
            for k in range(TCHUNKS):
                if k == 1:
                    sp.wait_ge(bias_zero, 1)
                    for q in range(3):
                        sp.dma_start(bias[32 * q:32 * q + 1, :], b_ih).then_inc(bias_in, 16)
                        sp.dma_start(bias[32 * q + 1:32 * q + 2, :], b_hh).then_inc(bias_in, 16)
                if k < TCHUNKS - 1:
                    sp.dma_start(stage(k).rearrange("p (h d) -> p h d", d=D),
                                 full[:, k * THI:(k + 1) * THI, :]).then_inc(table_in[k], 16)
                else:
                    sp.dma_start(stage(k)[:, 0:(THI - 1) * D].rearrange("p (h d) -> p h d", d=D),
                                 full[:, k * THI:HI - 1, :]).then_inc(table_in[k], 16)
                    sp.wait_ge(tail_zero, 1)
                    sp.dma_start(stage(k)[0:V - (HI - 1) * LO, (THI - 1) * D:THI * D],
                                 table[(HI - 1) * LO:V, :]).then_inc(table_in[k], 16)
            sp.wait_ge(bias_split, 3)
            sp.dma_start(wih_sb[:, :], w_ih).then_inc(wih_in, 16)
            sp.wait_ge(low_done, STAGED)
            sp.dma_start(whh[:, :], w_hh).then_inc(whh_in, 16)

            def next_raw(b, buf):
                sp.wait_ge(decoded, 2 * b + 2)
                load_raw(b + 2, buf)

            def keep_x(b, par, slot):
                sp.wait_ge(xT_out, b + 1)
                sp.dma_start(x_dram[slot], xT_new[:, par, :]).then_inc(xT_kept[par], 16)

            for b in range(3):
                next_raw(b, b % 2)
                if b == 2:
                    keep_x(0, 0, FIRST // 2)
            with sp.Fori(0, WARM_BLOCKS // 2 - 1) as i:
                for e in range(2):
                    next_raw(2 * i + e + 3, 1 - e)
                    keep_x(2 * i + e + 1, 1 - e, 2 * i + e + 1 + FIRST // 2)
            for b in range(WARM_BLOCKS + 1, BLOCKS + 2):
                if b + 2 < BLOCKS:
                    next_raw(b, b % 2)
                keep_x(b - 2, b % 2, (b - 2 + FIRST // 2) % (BLOCKS))

            def run(r, base):
                for m in range(2):
                    sp.dma_start(xT_old[:, m, :], x_dram[m]).then_inc(r.x_in[m], 16)
                with sp.Fori(1, L // 4) as i:
                    for m in range(2):
                        sp.wait_ge(r.full[1], base + 4 * i + 2 * m - 2)
                        sp.dma_start(xT_old[:, m, :], x_dram[2 * i + m]).then_inc(r.x_in[m], 16)

            for par in range(2):
                sp.wait_ge(xT_kept[par], 16 * (BLOCKS // 2))
            run(main, 0)
            with redo_needed(sp, 0):
                run(again, 0)
                with redo_needed(sp, 1):
                    with sp.Fori(1, CH - 1) as n:
                        sp.wait_ge(again.full[1], n * L)
                        run(again, n * L)
                sp.nop()
            sp.wait_ge(x_full, BLOCKS)
            sp.dma_start(w1_sb, w1.rearrange("p (k n) -> p k n", k=KH)).then_inc(head_in, 16)
            sp.dma_start(wo_sb, w_out.rearrange("p (k n) -> p k n", k=2)).then_inc(head_in, 16)
            sp.dma_start(b1_sb, b1).then_inc(head_in, 16)
            sp.dma_start(bo_sb[0:1, :], b_out).then_inc(head_in, 16)
            out_v = out.rearrange("(n p) c -> p n c", p=P)
            for n in range(4):
                sp.wait_ge(y_out, 4 * n + 4)
                sp.dma_start(out_v[:, 4 * n:4 * n + 4, :], out_sb[:, 4 * n:4 * n + 4, :]).then_inc(stored, 16)
            sp.wait_ge(stored, 16 * 4)

        @block.tensor
        def _(pe):
            def histogram(b, u, first_block=False):
                lo, hi = lo_codes(u % 2), hi_codes(u % 2)
                pe.wait_ge(codes_ready, b * UNITS + u + 1)
                if not (first_block and u < 2):
                    pe.wait_ge(counts_out, b * UNITS + u - 1)
                for r in range(UNIT):
                    at = HI * (r % 4)
                    for half in range(HALVES):
                        col = r * HALVES + half
                        mm = nc.tensor.matmul(ps[:, 2 * (u % 2) + r // 4, at:at + HI], lo[:, col, :], hi[:, col, :],
                                              start=(half == 0), stop=(half == HALVES - 1))
                mm.then_inc(counts_full, 1)

            def pool_slice(b, par, u, of, table_waits=False):
                if u == 0:
                    pe.wait_ge(counts_out, b * UNITS + UNITS)
                c = cnt(par)
                for hi in range(HI * u // of, HI * (u + 1) // of):
                    if table_waits and (hi % THI == 0 or hi == HI * u // of):
                        pe.wait_ge(low_done, hi // THI + 1)
                    mm = nc.tensor.matmul(ps[:, X_BANK + par, 0:3 * D], c[:, hi, :], parts(hi),
                                          start=(hi == 0), stop=(hi == HI - 1))
                if u == of - 1:
                    mm.then_inc(x_full, 1)

            def turn(b, par):
                pe.wait_ge(x_summed, b + 1)
                nc.tensor.transpose(ps[:, XT_BANK, par * BLOCK:(par + 1) * BLOCK], xparts[:, par, 0:D],
                                    ident[:, :]).then_inc(xT_full, 1)

            def quad(j):
                return slice(CH * j, CH * j + CH)

            def bias_part(place, seg):
                s, c0, n = seg
                for j in range(NJ):
                    nc.tensor.matmul(place(quad(j), s), biassel[:, :],
                                     bias3[:, j * 512 + c0:j * 512 + c0 + n], start=True, stop=False)

            def x_part(place, seg, x, ks=(0, 1)):
                s, c0, n = seg
                for k in ks:
                    for j in range(NJ):
                        nc.tensor.matmul(place(quad(j), s), x[:, CH * k:CH * k + CH],
                                         wih[:, k, j * 512 + c0:j * 512 + c0 + n], start=False, stop=False)

            def h_part(r, place, seg, par, ks=range(KH)):
                s, c0, n = seg
                for k in ks:
                    for j in range(NJ):
                        mm = nc.tensor.matmul(place(quad(j), s), hT[par][:, CH * k:CH * k + CH],
                                              whh_v[:, k, j * 512 + c0:j * 512 + c0 + n],
                                              start=False, stop=(k == KH - 1))
                if KH - 1 in ks:
                    mm.then_inc(r.full[s], 1)

            def turn_h(r, s):
                pe.wait_ge(r.h, s + 1)
                nc.tensor.transpose(hT_ps, h_now, ident[:, :]).then_inc(r.turned, 1)

            def turn_x(b, par):
                pe.wait_ge(x_summed, b + 1)
                nc.tensor.transpose(xT_ps(par), xparts[:, par, 0:D], ident[:, :]).then_inc(xT_full, 1)

            def beside(u, b, par, last):
                v, half = u % HALF, u // HALF
                s, place = 2 * b + half, early(1 - par)
                x = xT_new[:, par, half * 2 * CH:(half + 1) * 2 * CH]
                x_next = xT_new[:, half ^ par, (1 - half) * 2 * CH:(2 - half) * 2 * CH]
                if v == 0:
                    pe.wait_ge(warm.hT, s + 1)
                if v < KH:
                    h_part(warm, place, GIF, half, (v,))
                if v == 4:
                    if half == 0:
                        pe.wait_ge(x_out, b + 2)
                    else:
                        pe.wait_ge(warm.o, s)
                    bias_part(place, OUTG)
                    x_part(place, OUTG, x)
                if v == 5:
                    h_part(warm, place, OUTG, half)
                if v == 6 and not last:
                    pe.wait_ge(warm.gif, s + 1)
                    bias_part(place, GIF)
                    if half == 1:
                        pe.wait_ge(xT_out, b + 2)
                    x_part(place, GIF, x_next, (0,))
                if v == 7 and not last:
                    x_part(place, GIF, x_next, (1,))

            def body(b, par, table_waits=False, pool=True, turn=True, steps=True, last=False):
                for u in range(UNITS):
                    histogram(b, u, first_block=not pool)
                    if steps and u % HALF == HALF - 1:
                        turn_h(warm, 2 * (b - 3) + u // HALF)
                    if pool:
                        pool_slice(b - 1, 1 - par, u, UNITS, table_waits)
                    if steps:
                        beside(u, b - 3, 1 - par, last and u // HALF == 1)
                    if turn and u == 2:
                        turn_x(b - 2, par)

            body(0, 0, pool=False, turn=False, steps=False)
            pe.wait_ge(ident_set, 1)
            body(1, 1, table_waits=True, turn=False, steps=False)
            body(2, 0, steps=False)
            pe.wait_ge(bias_split, 3)
            pe.wait_ge(bias3_zero, 1)
            pe.wait_ge(biassel_set, 1)
            bias_part(early(0), GIF)
            pe.wait_ge(wih_in, 16)
            pe.wait_ge(xT_out, 1)
            x_part(early(0), GIF, xT_new[:, 0, 0:2 * CH])
            pe.wait_ge(whh_in, 16)
            with pe.Fori(0, WARM_BLOCKS // 2 - 1) as i:
                for e in range(2):
                    body(2 * i + e + 3, 1 - e)
            for b in range(WARM_BLOCKS + 1, WARM_BLOCKS + 3):
                body(b, b % 2, last=(b == WARM_BLOCKS + 2))
            for b in range(WARM_BLOCKS + 3, BLOCKS):
                body(b, b % 2, steps=False)
            pool_slice(BLOCKS - 1, 1, 0, 2)
            turn_x(BLOCKS - 2, 0)
            pool_slice(BLOCKS - 1, 1, 1, 2)
            turn_x(BLOCKS - 1, 1)

            def step(r, s, q, more):
                par = q % 2
                h_part(r, later(par), GIF, par)
                h_part(r, later(par), OUTG, par)
                if more is not None:
                    place = later(1 - par)
                    n = (q + 1) % 4
                    x = xT_old[:, n // 2, n % 2 * 2 * CH:(n % 2 + 1) * 2 * CH]
                    bias_part(place, OUTG)
                    bias_part(place, GIF)
                    if n % 2 == 0:
                        pe.wait_ge(r.x_in[n // 2], more)
                    x_part(place, OUTG, x)
                    x_part(place, GIF, x, (0,))
                turn_h(r, s)
                if more is not None:
                    x_part(place, GIF, x, (1,))
                    pe.wait_ge(r.hT, s + 1)

            def run(r, base, turns, begin):
                bias_part(later(0), OUTG)
                bias_part(later(0), GIF)
                pe.wait_ge(r.x_in[0], turns + 16)
                x_part(later(0), OUTG, xT_old[:, 0, 0:2 * CH])
                x_part(later(0), GIF, xT_old[:, 0, 0:2 * CH])
                begin()
                with pe.Fori(0, L // 4 - 1) as i:
                    for q in range(4):
                        step(r, base + 4 * i + q, q, turns + 16 * i + (32 if q == 3 else 16))
                for q in range(4):
                    step(r, base + L - 4 + q, q, turns + 4 * L if q < 3 else None)

            def seam(done):
                nc.tensor.matmul(ps[:, S_BANK, 0:P], shift[:, :], c_now, start=True, stop=True)
                nc.tensor.matmul(ps[:, S_BANK, P:2 * P], h_now, shift[:, :], start=True, stop=True).then_inc(done, 1)

            pe.wait_ge(shift_set, 1)
            seam(seam1)
            run(main, 0, 0, lambda: pe.wait_ge(seam1_set, 1))

            def vote(n):
                seam(seam2)
                pe.wait_ge(compare, n + 1)
                nc.tensor.matmul(ps[0:1, S_BANK, 2 * P:2 * P + 1], agree_row, ones[:, 0:1], start=True, stop=True)\
                    .then_inc(agree_sum, 1)

            vote(0)
            pe.wait_ge(main.kept, L + 2)
            with redo_needed(pe, 0):
                pe.wait_ge(restarted, 1)
                run(again, 0, 0, lambda: None)
                vote(1)
                pe.wait_ge(again.kept, L + 2)
                with redo_needed(pe, 1):
                    with pe.Fori(1, CH - 1) as n:
                        seam(seam2)
                        pe.wait_ge(restarted, n + 1)
                        run(again, n * L, n * 4 * L, lambda: None)
                    pe.wait_ge(again.kept, (CH - 1) * L + 2)
                pe.nop()
            pe.wait_ge(head_in, 64)

            def hidden(n):
                for m in range(2):
                    q = 2 * n + m
                    if q >= 4:
                        pe.wait_ge(h1_ready, q - 3)
                    for k in range(KH):
                        mm = nc.tensor.matmul(ps[:, q % 4, :], w1_sb[:, k, m * P:(m + 1) * P],
                                              hs_flat[:, k, 512 * n:512 * n + 512],
                                              start=(k == 0), stop=(k == KH - 1))
                    mm.then_inc(h1_full, 1)

            def head(n):
                pe.wait_ge(h1_ready, 2 * n + 2)
                for t in range(4):
                    y = 4 * n + t
                    if y >= 2:
                        pe.wait_ge(y_out, y - 1)
                    o = ps[:, 4 + y % 2, 0:C]
                    nc.tensor.matmul(o, ones[0:1, :], bo_sb[0:1, :], start=True, stop=False)
                    for m in range(2):
                        mm = nc.tensor.matmul(o, h1[n % 2][:, m, P * t:P * t + P], wo_sb[:, m, :],
                                              start=False, stop=(m == 1))
                    mm.then_inc(y_full, 1)

            hidden(0)
            for n in range(4):
                if n < 3:
                    hidden(n + 1)
                head(n)

        @block.scalar
        def _(act):
            def split(step):
                if step < TCHUNKS:
                    act.wait_ge(table_in[step], 32 if step == TCHUNKS - 1 else 16)
                    nc.scalar.activation(tpart(0, step), stage_v(step), ACT.Copy).then_inc(top_done, 1)
                if 0 <= step - 1 < TCHUNKS:
                    act.wait_ge(rest1_done, step)
                    nc.scalar.activation(tpart(1, step - 1), stage_v(step - 1), ACT.Copy).then_inc(mid_done, 1)
                if 0 <= step - 2 < TCHUNKS:
                    act.wait_ge(rest2_done, step - 1)
                    nc.scalar.activation(tpart(2, step - 2), stage_v(step - 2), ACT.Copy).then_inc(low_done, 1)

            def take_counts(b, par, g):
                act.wait_ge(counts_full, b * UNITS + g + 1)
                at = ps[:, 2 * (g % 2):2 * (g % 2) + 2, 0:4 * HI].rearrange("p b (r h) -> p h b r", h=HI)
                nc.scalar.activation(cnt(par)[:, :, g * UNIT:(g + 1) * UNIT].rearrange("p h (b r) -> p h b r", b=2),
                                     at, ACT.Copy).then_inc(counts_out, 1)

            def x_rows_out(b, par):
                act.wait_ge(x_full, b + 1)
                nc.scalar.activation(xparts[:, par, :], ps[:, X_BANK + par, 0:3 * D], ACT.Copy,
                                     scale=1.0 / MEAN_OVER).then_inc(x_out, 1)

            def x_turned_out(b, par):
                act.wait_ge(xT_full, b + 1)
                nc.scalar.activation(xT_new[:, par, :], xT_ps(par), ACT.Copy).then_inc(xT_out, 1)

            def act_gif(r, s, place):
                act.wait_ge(r.full[0], s + 1)
                nc.scalar.activation(sig_if, place(EVERY, 0)[:, P:3 * P], ACT.Sigmoid)
                nc.scalar.activation(tanh_g, place(EVERY, 0)[:, 0:P], ACT.Tanh).then_inc(r.gif, 1)

            def act_o(r, s, place):
                act.wait_ge(r.full[1], s + 1)
                nc.scalar.activation(sig_o, place(EVERY, 1), ACT.Sigmoid).then_inc(r.o, 1)

            def act_c(r, s):
                act.wait_ge(r.c, s + 1)
                nc.scalar.activation(tanh_c, c_now, ACT.Tanh).then_inc(r.tc, 1)

            def body(b, par, turn=True, steps=True, stored=None, parts=False):
                if turn:
                    x_rows_out(b - 2, par)
                for u in range(UNITS):
                    if parts and u % 2 == 0:
                        split(u // 2)
                    take_counts(b, par, u)
                    if turn and u == 3:
                        if stored is not None:
                            act.wait_ge(xT_kept[par], stored)
                        x_turned_out(b - 2, par)
                    if steps:
                        s = 2 * (b - 3) + u // HALF
                        if u % HALF == 3:
                            act_gif(warm, s, early(par))
                        if u % HALF == 5:
                            act_c(warm, s)
                            act_o(warm, s, early(par))
                        if u % HALF == 7:
                            act.wait_ge(warm.turned, s + 1)
                            nc.scalar.activation(hT[1 - u // HALF], hT_ps, ACT.Copy).then_inc(warm.hT, 1)

            act.wait_ge(ones_set, 1)
            nc.scalar.activation(xparts[:, 0, 0:1], ones[:, 0:1], ACT.Sigmoid)
            nc.scalar.activation(hT[0], ones[:, :], ACT.Copy, scale=0.0).then_inc(warm.hT, 1)
            act.wait_ge(bias_in, 16 * 6)
            nc.scalar.activation(bias3[0:96, :], bias[0:96, :], ACT.Copy).then_inc(bias_split, 1)
            act.wait_ge(bias_rest, 1)
            nc.scalar.activation(bias3[32:64, :], bias[32:64, :], ACT.Copy)
            nc.scalar.activation(bias3[64:96, :], bias[64:96, :], ACT.Copy).then_inc(bias_split, 1)
            act.wait_ge(bias_rest, 2)
            nc.scalar.activation(bias3[64:96, :], bias[64:96, :], ACT.Copy).then_inc(bias_split, 1)
            body(0, 0, turn=False, steps=False, parts=True)
            split(UNITS // 2)
            act.wait_ge(low_done, TCHUNKS)
            body(1, 1, turn=False, steps=False)
            body(2, 0, steps=False)
            body(3, 1)
            with act.Fori(0, WARM_BLOCKS // 2 - 1) as i:
                for e in range(2):
                    body(2 * i + e + 4, e, stored=16 * i + 16)
            body(WARM_BLOCKS + 2, 0, stored=8 * WARM_BLOCKS)
            for b in range(WARM_BLOCKS + 3, BLOCKS):
                body(b, b % 2, steps=False, stored=16 * ((b - 2) // 2))
            for par in range(2):
                x_rows_out(BLOCKS - 2 + par, par)
                act.wait_ge(xT_kept[par], 16 * (BLOCKS // 2 - 1))
                x_turned_out(BLOCKS - 2 + par, par)

            def run(r, base):
                with act.Fori(0, L // 2) as i:
                    for par in range(2):
                        s = base + 2 * i + par
                        act_gif(r, s, later(par))
                        act_o(r, s, later(par))
                        act_c(r, s)

            run(main, 0)
            with redo_needed(act, 0):
                run(again, 0)
                with redo_needed(act, 1):
                    with act.Fori(1, CH - 1) as n:
                        run(again, n * L)
                act.nop()
            act.wait_ge(head_in, 64)
            for n in range(4):
                if n >= 2:
                    act.wait_ge(y_full, 4 * (n - 1))
                for m in range(2):
                    q = 2 * n + m
                    act.wait_ge(h1_full, q + 1)
                    nc.scalar.activation(h1[n % 2][:, m, :], ps[:, q % 4, :], ACT.Relu,
                                         bias=b1_sb[:, m:m + 1]).then_inc(h1_ready, 1)

        @block.vector
        def _(dve):
            nc.vector.memset(biassel[:, :], 0.0).then_inc(biassel_zero, 1)
            dve.wait_ge(biassel_zero, 1)
            for q in range(3):
                last = nc.vector.memset(biassel[32 * q:32 * q + 2, :], 1.0)
            last.then_inc(biassel_set, 1)
            dve.wait_ge(ramp_ready, 1)
            nc.vector.tensor_copy(ramp[:, :], ramp32).then_inc(ramp_ready, 1)
            dve.wait_ge(ramp_ready, 2)

            def decode(b, buf):
                dve.wait_ge(raw_in[buf], 16 * b + 16)
                low16 = raw[:, buf, :].bitcast(I16).rearrange("p (c e) -> p c e", e=2)[:, :, 0:1]\
                    .to_broadcast([P, BLOCK * HALVES, 2])
                nc.vector.tensor_scalar(lo2[:, :, :], low16, LO - 1, None, ALU.bitwise_and).then_inc(decoded, 1)
                nc.vector.tensor_scalar(hi2[:, :, :], low16, 7, None, ALU.logical_shift_right).then_inc(decoded, 1)

            def one_hot(codes_v, n, pairs, u):
                c = pairs[:, UC * u:UC * u + UC, :].unsqueeze(2).to_broadcast([P, UC, n // 2, 2])
                r = ramp[:, 0:n].rearrange("p (v e) -> p v e", e=2).unsqueeze(1).to_broadcast([P, UC, n // 2, 2])
                return nc.vector.tensor_tensor(codes_v.rearrange("p c (v e) -> p c v e", e=2), c, r, ALU.is_equal)

            def dve_c(r, s):
                dve.wait_ge(r.gif, s + 1)
                nc.vector.tensor_tensor(products, sig_if, gc, ALU.mult).then_inc(r.terms, 1)
                dve.wait_ge(r.terms, s + 1)
                nc.vector.tensor_tensor(c_now, products[:, 0:P], products[:, P:2 * P], ALU.add).then_inc(r.c, 1)

            def dve_h(r, s):
                dve.wait_ge(r.o, s + 1)
                dve.wait_ge(r.tc, s + 1)
                nc.vector.tensor_tensor(h_now, sig_o, tanh_c, ALU.mult).then_inc(r.h, 1)

            def dve_hT(r, s, par):
                if r.keep:
                    dve.wait_ge(r.kept, s + 1)
                dve.wait_ge(r.turned, s + 1)
                nc.vector.tensor_copy(hT[1 - par], hT_ps).then_inc(r.hT, 1)

            def body(b, buf, turn, steps=True, first=False):
                if not first:
                    dve.wait_ge(codes_ready, b * UNITS)
                decode(turn, buf)
                dve.wait_ge(decoded, 2 * b + 2)
                for u in range(UNITS):
                    if not (first and u < 2):
                        dve.wait_ge(counts_full, b * UNITS + u - 1)
                    one_hot(lo_codes(u % 2), LO, lo2, u)
                    one_hot(hi_codes(u % 2), HI, hi2, u).then_inc(codes_ready, 1)
                    if steps:
                        s = 2 * (b - 3) + u // HALF
                        if u % HALF == 6:
                            dve_c(warm, s)
                        if u % HALF == 7:
                            dve_h(warm, s)

            nc.vector.memset(c_now, 0.0).then_inc(warm_c_zero, 1)
            nc.vector.memset(bias3[96:128, :], 0.0).then_inc(bias3_zero, 1)
            body(0, 0, 0, steps=False, first=True)
            body(1, 1, 0, steps=False)
            body(2, 0, 1, steps=False)
            dve.wait_ge(warm_c_zero, 1)
            with dve.Fori(0, WARM_BLOCKS // 2) as i:
                for e in range(2):
                    body(2 * i + e + 3, 1 - e, i + 1 + e)
            for b in range(WARM_BLOCKS + 3, BLOCKS):
                body(b, b % 2, b // 2, steps=False)

            def run(r, base):
                with dve.Fori(0, L // 2) as i:
                    for par in range(2):
                        s = base + 2 * i + par
                        dve_c(r, s)
                        dve_h(r, s)
                        dve_hT(r, s, par)

            def from_seam(done):
                nc.vector.tensor_copy(c_now, ps[:, S_BANK, 0:P])
                nc.vector.tensor_copy(hT[0], ps[:, S_BANK, P:2 * P])
                nc.vector.tensor_copy(start, ps[:, S_BANK, 0:2 * P]).then_inc(done, 1)

            def vote(n):
                dve.wait_ge(seam2, n + 1)
                nc.vector.tensor_tensor(diff, ps[:, S_BANK, 0:2 * P], start, ALU.subtract).then_inc(compare_step, 1)
                dve.wait_ge(compare_step, 3 * n + 1)
                nc.vector.tensor_tensor(sq, diff, diff, ALU.mult).then_inc(compare_step, 1)
                dve.wait_ge(compare_step, 3 * n + 2)
                nc.vector.tensor_scalar(agree, sq, TOL * TOL, None, ALU.is_le).then_inc(compare_step, 1)
                dve.wait_ge(compare_step, 3 * n + 3)
                nc.vector.tensor_reduce(agree_row, agree, AX.X, ALU.add).then_inc(compare, 1)
                dve.wait_ge(agree_sum, n + 1)
                nc.vector.tensor_scalar(redo[0:1, :], ps[0:1, S_BANK, 2 * P:2 * P + 1], float(2 * P * P), None, ALU.is_lt)\
                    .then_inc(redo_set, 1)

            dve.wait_ge(seam1, 1)
            dve.wait_ge(warm.hT, WARM + 1)
            from_seam(seam1_set)
            run(main, 0)
            vote(0)
            with redo_needed(dve, 0):
                dve.wait_ge(main.kept, L + 2)
                from_seam(restarted)
                run(again, 0)
                vote(1)
                with redo_needed(dve, 1):
                    with dve.Fori(1, CH - 1) as n:
                        dve.wait_ge(again.kept, n * L + 2)
                        dve.wait_ge(seam2, n + 2)
                        from_seam(restarted)
                        run(again, n * L)
                dve.nop()

            for y in range(T // P):
                dve.wait_ge(y_full, y + 1)
                nc.vector.tensor_copy(out_sb[:, y, :], ps[:, 4 + y % 2, 0:C]).then_inc(y_out, 1)

        @block.gpsimd
        def _(pool):
            nc.gpsimd.memset(bias, 0.0).then_inc(bias_zero, 1)
            nc.gpsimd.iota(ramp32, pattern=[[1, LO]], base=0, channel_multiplier=0).then_inc(ramp_ready, 1)
            nc.gpsimd.memset(stage(TCHUNKS - 1)[:, (THI - 1) * D:THI * D], 0.0).then_inc(tail_zero, 1)
            nc.gpsimd.memset(ident[:, :], 0.0).then_inc(blank, 1)
            nc.gpsimd.memset(shift[:, :], 0.0).then_inc(blank, 1)
            nc.gpsimd.memset(ones[:, :], 1.0).then_inc(ones_set, 1)
            pool.wait_ge(blank, 2)
            nc.gpsimd.affine_select(out=ident[:, :], in_=ident[:, :], compare_op=ALU.not_equal, fill=1.0,
                                    base=0, pattern=[[-1, P]], channel_multiplier=1).then_inc(ident_set, 1)
            nc.gpsimd.affine_select(out=shift[:, :], in_=shift[:, :], compare_op=ALU.not_equal, fill=1.0,
                                    base=1, pattern=[[-1, P]], channel_multiplier=1).then_inc(blank, 1)
            pool.wait_ge(blank, 3)
            nc.gpsimd.memset(shift[:, :].rearrange("p (j c) -> p j c", c=CH)[:, :, 0:1], 0.0).then_inc(shift_set, 1)

            def rest(n, k, wait, done):
                pool.wait_ge(wait, k + 1)
                nc.gpsimd.tensor_tensor(stage_v(k), stage_v(k), tpart(n, k), ALU.subtract).then_inc(done, 1)

            for part_n, rows in enumerate((slice(0, 96), slice(64, 96))):
                pool.wait_ge(bias_split, part_n + 1)
                nc.gpsimd.tensor_tensor(bias[rows, :], bias[rows, :], bias3[rows, :], ALU.subtract).then_inc(bias_rest, 1)
            for step in range(TCHUNKS + 1):
                if step < TCHUNKS:
                    rest(0, step, top_done, rest1_done)
                if step >= 1:
                    rest(1, step - 1, mid_done, rest2_done)

            def sum_parts(b, par):
                pool.wait_ge(x_out, b + 1)
                top, mid, low = (xparts[:, par, n * D:(n + 1) * D] for n in range(3))
                nc.gpsimd.tensor_tensor(mid, mid, low, ALU.add).then_inc(x_half, 1)
                pool.wait_ge(x_half, b + 1)
                nc.gpsimd.tensor_tensor(top, top, mid, ALU.add).then_inc(x_summed, 1)

            with pool.Fori(0, BLOCKS // 2) as i:
                for par in range(2):
                    sum_parts(2 * i + par, par)

            def keep(r, l, par):
                if r.keep:
                    nc.gpsimd.tensor_copy(hs[:, :, :, bass.ds(l, 1)],
                                          hT[1 - par].rearrange("p (k c) -> p k c", k=KH).unsqueeze(3))\
                        .then_inc(r.kept, 1)

            def keep_last(r, l, par):
                if r.keep:
                    h = hT[1 - par].rearrange("p (k c) -> p k c", k=KH).unsqueeze(3)
                    one = ones[:, :].rearrange("p (k c) -> p k c", k=KH).unsqueeze(3)
                    nc.gpsimd.tensor_tensor(hs[:, :, :, l:l + 1], h, one, ALU.mult).then_inc(r.kept, 1)

            def run(r, base):
                with pool.Fori(0, L // 2 - 1) as i:
                    for par in range(2):
                        pool.wait_ge(r.hT, base + 2 * i + par + 1)
                        keep(r, 2 * i + par, par)
                for par in range(2):
                    pool.wait_ge(r.hT, base + L - 1 + par)
                    keep_last(r, L - 2 + par, par)

            pool.sem_inc(main.kept, 2)
            run(main, 0)
            with redo_needed(pool, 0):
                pool.sem_inc(again.kept, 2)
                run(again, 0)
                with redo_needed(pool, 1):
                    with pool.Fori(1, CH - 1) as n:
                        run(again, n * L)
                pool.nop()


def kernel(r_diag_idx, r_proc_idx, L0_rec_embedding, L0_rec_W_ih, L0_rec_W_hh, L0_rec_b_ih, L0_rec_b_hh,
           L0_rec_W1, L0_rec_b1, L0_rec_W_out, L0_rec_b_out):
    import numpy as np
    import concourse.bacc as bacc
    from concourse.bass_utils import run_bass_kernel_spmd

    def a(x):
        return np.asarray(x)

    idx = np.stack([a(r_diag_idx), a(r_proc_idx)]).reshape(2, CH, BLOCKS, 2, HALVES, P)
    idx = np.roll(idx.transpose(2, 5, 3, 0, 1, 4), -(FIRST // 2), axis=0)
    order = [2, 0, 1, 3]

    def gates(w):
        return w.reshape(4, NJ, P, -1)[order].transpose(1, 0, 2, 3).reshape(G4, -1)

    def tall(w):
        n = w.shape[0]
        return w.reshape(n, -1, P).transpose(2, 1, 0).reshape(P, -1)

    arrays = {
        "raw_idx": idx.reshape(BLOCKS, P, BLOCK * HALVES),
        "table": a(L0_rec_embedding),
        "w_ih": tall(gates(a(L0_rec_W_ih))),
        "w_hh": tall(gates(a(L0_rec_W_hh))),
        "b_ih": gates(a(L0_rec_b_ih)).reshape(1, G4),
        "b_hh": gates(a(L0_rec_b_hh)).reshape(1, G4),
        "w1": tall(a(L0_rec_W1)),
        "b1": a(L0_rec_b1).reshape(2, P).T,
        "w_out": tall(a(L0_rec_W_out)),
        "b_out": a(L0_rec_b_out).reshape(1, C),
    }
    arrays = {name: np.ascontiguousarray(x) for name, x in arrays.items()}
    nc = bacc.Bacc("TRN2", target_bir_lowering=False, num_devices=1)
    args = [nc.dram_tensor(name, x.shape, mybir.dt.from_np(x.dtype), kind="ExternalInput").ap()
            for name, x in arrays.items()]
    out = nc.dram_tensor("out", (T, C), F32, kind="ExternalOutput").ap()
    lstm_kernel(nc, *args, out)
    got = run_bass_kernel_spmd(nc, [arrays], core_ids=[0])
    return got.results[0]["out"]
```

```python
from contextlib import ExitStack

import concourse.bass as bass
from concourse import mybir

ALU = mybir.AluOpType
ACT = mybir.ActivationFunctionType
AX = mybir.AxisListType
F32 = mybir.dt.float32
BF16 = mybir.dt.bfloat16
I32 = mybir.dt.int32
I16 = mybir.dt.int16

P = 128
T = 2048
V, D = 12500, 128
POOLED = 256
MEAN_OVER = 8
HALVES = POOLED // P
ROWS = 2 * T
LO = 128
HI = -(-V // LO)
BLOCK = 128
BLOCKS = ROWS // BLOCK
UNIT = 8
UNITS = BLOCK // UNIT
CODE = LO + HI
TCHUNKS = 7
THI = HI // TCHUNKS
STAGED = 4
GROUP = 4

H = 512
G4 = 4 * H
KH = H // P
NJ = H // P
CH = 32
L = T // CH
WARM = 52
TOL = 2.0 ** -19
GROUPS = L // GROUP
LAST = GROUPS - 1
H2 = 256
C = 100
FIRST = L - WARM
WARM_BLOCKS = WARM // 2
HALF = UNITS // 2
FIRST_STEPS = 3
WARM_END = FIRST_STEPS + WARM_BLOCKS
SPLIT_AT = [[7 * (k // 2) + at[k % 2] for k in range(TCHUNKS)] for at in ((-2, 0), (1, 4), (6, 9))]
GIF, OUTG = (0, 0, 384), (1, 384, 128)


def lstm_kernel(nc, raw_idx, table, w_ih, w_hh, b_ih, b_hh, w1, b1, w_out, b_out, out):
    ctx = ExitStack()
    with ctx:
        def sb(name, shape, dt):
            return ctx.enter_context(nc.sbuf_tensor(name, shape, dt))

        def sem(name):
            return ctx.enter_context(nc.semaphore(name))

        tparts = sb("tparts", [P, 3 * HI * D], BF16)
        counts = sb("counts", [P, 2 * HI * BLOCK], BF16)
        codes = sb("codes", [P, 2 * UNIT * HALVES * CODE], BF16)
        whh = sb("whh", [P, KH * G4], F32)
        wih_sb = sb("wih", [P, 2 * G4], F32)
        bias = sb("bias", [P, 4 * P], F32)
        raw = sb("raw", [P, 2, BLOCK * HALVES], I32)
        lo2 = sb("lo2", [P, BLOCK * HALVES, 2], I16)
        hi2 = sb("hi2", [P, BLOCK * HALVES, 2], I16)
        ramp = sb("ramp", [P, LO], I16)
        ramp32 = counts[:, 0:2 * LO].bitcast(I32)
        ident = sb("ident", [P, P], F32)
        shift = sb("shift", [P, P], F32)
        ones = sb("ones", [P, P], F32)
        xparts = sb("xparts", [P, 2, 3 * D], F32)
        xT_new = sb("xT_new", [P, 2, BLOCK], F32)
        gx_new = sb("gx_new", [P, 2, 4 * P], F32)

        tparts_v = tparts[:, :].rearrange("p (h n d) -> p h n d", n=3, d=D)

        def parts(hi):
            return tparts[:, hi * 3 * D:(hi + 1) * 3 * D]

        def tpart(n, k):
            return tparts_v[:, k * THI:(k + 1) * THI, n, :]

        def cnt(buf):
            return counts[:, buf * HI * BLOCK:(buf + 1) * HI * BLOCK].rearrange("p (h r) -> p h r", r=BLOCK)

        UC = UNIT * HALVES

        def lo_codes(buf):
            at = buf * UC * CODE
            return codes[:, at:at + UC * LO].rearrange("p (c v) -> p c v", v=LO)

        def hi_codes(buf):
            at = buf * UC * CODE + UC * LO
            return codes[:, at:at + UC * HI].rearrange("p (c v) -> p c v", v=HI)

        SW = THI * D
        first_stage = counts[:, HI * BLOCK:HI * BLOCK + 2 * (TCHUNKS - STAGED) * SW].bitcast(F32)

        def stage(k):
            if k < TCHUNKS - STAGED:
                return first_stage[:, k * SW:(k + 1) * SW]
            k -= TCHUNKS - STAGED
            return whh[:, k * SW:(k + 1) * SW]

        def stage_v(k):
            return stage(k).rearrange("p (h d) -> p h d", d=D)

        wih = wih_sb[:, :].rearrange("p (k n) -> p k n", k=2)
        hs = counts[:, 0:2 * KH * T].bitcast(F32).rearrange("p (l kc) -> p l kc", l=L)
        rest = tparts[:, :].bitcast(F32)
        taken = [0]

        def carve(n):
            taken[0] += n
            return rest[:, taken[0] - n:taken[0]]

        def tile(name, n):
            return sb(name, [P, n], F32)[:, :]

        gc = tile("gc", 2 * P)
        sig_if = tile("sig_if", 2 * P)
        products = tile("products", 2 * P)
        tanh_g, c_now = gc[:, 0:P], gc[:, P:2 * P]
        tanh_c = products[:, 0:P]
        sig_o, h_now = (tile(name, P) for name in ("sig_o", "h_now"))
        hT = [tile(f"hT{i}", P) for i in range(2)]
        start = carve(2 * P)
        gx_old = carve(GROUP * 4 * P).rearrange("p (m n) -> p m n", m=GROUP)
        diff = carve(2 * P)
        sq = carve(2 * P)
        agree = carve(2 * P)
        agree_row = carve(1)
        redo = carve(1).bitcast(I32)
        w1_sb = carve(KH * H2).rearrange("p (k n) -> p k n", k=KH)
        wo_sb = carve(2 * C).rearrange("p (k n) -> p k n", k=2)
        b1_sb = carve(2)
        bo_sb = carve(C)
        h1 = carve(2 * P).rearrange("p (m n) -> p m n", m=2)
        y_sb = carve(C)
        whh_v = whh[:, :].rearrange("p (k n) -> p k n", k=KH)

        ps = ctx.enter_context(nc.psum_tensor("ps", [P, 8, 512], F32))
        X_BANK = 4
        T_BANK = 6
        S_BANK = 7

        def xT_ps(par):
            return ps[:, T_BANK, par * BLOCK:(par + 1) * BLOCK]

        hT_ps = ps[:, T_BANK, 2 * P:3 * P]
        seam_ps = ps[:, T_BANK, 2 * P:4 * P]
        votes_ps = ps[0:1, S_BANK, P:P + 1]
        h1_ps = ps[:, X_BANK:X_BANK + 2, 0:P]
        y_ps = ps[:, S_BANK, 0:C]

        def early(par):
            return lambda rows, s: ps[rows, S_BANK, 0:3 * P] if s == 0 else ps[rows, X_BANK + par, 3 * P:4 * P]

        def later(par):
            return lambda rows, s: ps[rows, 2 * par + s, 0:(3 * P if s == 0 else P)]

        EVERY = slice(0, P)

        raw_in = [sem(f"raw_in{i}") for i in range(2)]
        decoded = sem("decoded")
        codes_ready = sem("codes_ready")
        counts_full = sem("counts_full")
        counts_out = sem("counts_out")
        x_full = sem("x_full")
        x_out = sem("x_out")
        x_half = sem("x_half")
        x_summed = sem("x_summed")
        xT_full = sem("xT_full")
        xT_out = sem("xT_out")
        gx_full = sem("gx_full")
        gx_copied = sem("gx_copied")
        gx_out = sem("gx_out")
        gx_kept = [sem(f"gx_kept{i}") for i in range(2)]
        table_in = [sem(f"table_in{k}") for k in range(TCHUNKS)]
        tail_zero = sem("tail_zero")
        top_done, mid_done, low_done = sem("top_done"), sem("mid_done"), sem("low_done")
        rest1_done, rest2_done = sem("rest1_done"), sem("rest2_done")
        ones_set, ident_set, shift_set = (sem(x) for x in ("ones_set", "ident_set", "shift_set"))
        ramp_ready = sem("ramp_ready")
        blank = sem("blank")
        whh_in, wih_in, bias_in, head_in = sem("whh_in"), sem("wih_in"), sem("bias_in"), sem("head_in")
        bias_ready = sem("bias_ready")
        warm_c_zero = sem("warm_c_zero")
        seam1 = sem("seam1")
        seam1_set = sem("seam1_set")
        seam2 = sem("seam2")
        compare = sem("compare")
        compare_step = sem("compare_step")
        agree_sum = sem("agree_sum")
        redo_set = sem("redo_set")
        restarted = sem("restarted")
        start_kept = sem("start_kept")

        gx_dram = nc.dram_tensor("gx_dram", (L, P, 4 * P), F32, kind="Internal").ap()

        class Run:

            def __init__(self, name, keep):
                self.keep = keep
                self.x_in = [sem(f"{name}_x_in{i}") for i in range(GROUP)]
                self.full = [sem(f"{name}_full{s}") for s in range(2)]
                self.gates = self.full if keep else [sem(f"{name}_gates{s}") for s in range(2)]
                self.gif = sem(name + "_gif")
                self.tc = sem(name + "_tc")
                self.o = sem(name + "_o")
                self.terms = sem(name + "_terms")
                self.c = sem(name + "_c")
                self.h = sem(name + "_h")
                self.turned = sem(name + "_turned")
                self.hT = sem(name + "_hT")
                if keep:
                    self.kept = sem(name + "_kept")
                    self.h1_full = sem(name + "_h1_full")
                    self.h1 = sem(name + "_h1")
                    self.y_full = sem(name + "_y_full")
                    self.y_out = sem(name + "_y_out")
                    self.stored = sem(name + "_stored")

        warm = Run("warm", False)
        main = Run("main", True)
        again = Run("again", True)

        def redo_needed(eng, n):
            eng.wait_ge(redo_set, n + 1)
            return eng.If(eng.value_load(redo[0:1, 0:1], min_val=0, max_val=1) > 0)

        block = ctx.enter_context(nc.Block())

        @block.sync
        def _(sp):
            def load_raw(b, buf):
                sp.dma_start(raw[:, buf, :], raw_idx[b]).then_inc(raw_in[buf], 16)

            load_raw(0, 0)
            load_raw(1, 1)
            full = table[0:(HI - 1) * LO, :].rearrange("(h l) d -> l h d", l=LO)
            for k in range(TCHUNKS):
                if k == 1:
                    for j in range(NJ):
                        for b, at in ((b_ih, bias), (b_hh, gx_new[:, 0, :])):
                            sp.dma_start(at[CH * j:CH * j + CH, :],
                                         b[0:1, j * 4 * P:(j + 1) * 4 * P].to_broadcast([CH, 4 * P]))\
                                .then_inc(bias_in, 16)
                if k < TCHUNKS - 1:
                    sp.dma_start(stage(k).rearrange("p (h d) -> p h d", d=D),
                                 full[:, k * THI:(k + 1) * THI, :]).then_inc(table_in[k], 16)
                else:
                    sp.dma_start(stage(k)[:, 0:(THI - 1) * D].rearrange("p (h d) -> p h d", d=D),
                                 full[:, k * THI:HI - 1, :]).then_inc(table_in[k], 16)
                    sp.wait_ge(tail_zero, 1)
                    sp.dma_start(stage(k)[0:V - (HI - 1) * LO, (THI - 1) * D:THI * D],
                                 table[(HI - 1) * LO:V, :]).then_inc(table_in[k], 16)
            def next_raw(b, buf):
                sp.wait_ge(decoded, 2 * b + 2)
                load_raw(b + 2, buf)

            def keep_gx(s, buf, step):
                sp.wait_ge(gx_out, 2 * s + 2)
                sp.dma_start(gx_dram[step], gx_new[:, buf, :]).then_inc(gx_kept[buf], 16)

            for b in range(3):
                next_raw(b, b % 2)
                if b == 0:
                    sp.dma_start(wih_sb[:, :], w_ih).then_inc(wih_in, 16)
                if b == 1:
                    sp.wait_ge(low_done, TCHUNKS)
                    sp.dma_start(whh[:, :], w_hh).then_inc(whh_in, 16)
            with sp.Fori(0, WARM_BLOCKS // 2) as i:
                for e in range(2):
                    next_raw(2 * i + e + 3, 1 - e)
                    for half in range(2):
                        s = 2 * (2 * i + e) + half
                        keep_gx(s, half, s + FIRST)

            def keep_rest(b):
                for half in range(2):
                    keep_gx(2 * b + half, half, 2 * (b - WARM_BLOCKS) + half)

            for b in range(WARM_BLOCKS, BLOCKS - 1):
                if b + 5 < BLOCKS:
                    next_raw(b + 3, (b + 3) % 2)
                keep_rest(b)

            def load_gx(r, step, m):
                sp.dma_start(gx_old[:, m, :], gx_dram[step]).then_inc(r.x_in[m], 16)

            y_rows = out.rearrange("(c g l) d -> g l c d", c=CH, l=GROUP)

            def store_y(r, base, g):
                sp.wait_ge(r.y_out, base + g + 1)
                sp.dma_start(y_rows[g], y_sb).then_inc(r.stored, 16)

            def run(r, base, first=lambda: None):
                for m in range(GROUP):
                    load_gx(r, m, m)
                first()

                def loads(i):
                    for m in range(GROUP):
                        sp.wait_ge(r.full[1], GROUP * (base + i) + m - (GROUP - 1))
                        load_gx(r, GROUP * i + m, m)

                loads(1)
                with sp.Fori(2, GROUPS) as i:
                    loads(i)
                    store_y(r, base, i - 2)
                for g in (GROUPS - 2, GROUPS - 1):
                    store_y(r, base, g)

            def beside_first_loads():
                keep_rest(BLOCKS - 1)
                sp.dma_start(w1_sb, w1.rearrange("p (k n) -> p k n", k=KH)).then_inc(head_in, 16)
                sp.dma_start(wo_sb, w_out.rearrange("p (k n) -> p k n", k=2)).then_inc(head_in, 16)
                sp.dma_start(b1_sb, b1).then_inc(head_in, 16)
                sp.dma_start(bo_sb[0:1, :], b_out).then_inc(head_in, 16)
                for buf in range(2):
                    sp.wait_ge(gx_kept[buf], 16 * BLOCKS)

            sp.wait_ge(x_full, BLOCKS)
            for buf in range(2):
                sp.wait_ge(gx_kept[buf], 16 * (WARM_BLOCKS + GROUP // 2))
            run(main, 0, beside_first_loads)
            sp.wait_ge(main.stored, 16 * GROUPS)
            with redo_needed(sp, 0):
                run(again, 0)
                sp.wait_ge(again.stored, 16 * GROUPS)
                with redo_needed(sp, 1):
                    with sp.Fori(1, CH - 1) as n:
                        run(again, n * GROUPS)
                    sp.wait_ge(again.stored, 16 * GROUPS * (CH - 1))
                sp.nop()

        @block.tensor
        def _(pe):
            def histogram(b, u, first_block=False):
                lo, hi = lo_codes(u % 2), hi_codes(u % 2)
                pe.wait_ge(codes_ready, b * UNITS + u + 1)
                if not (first_block and u < 2):
                    pe.wait_ge(counts_out, b * UNITS + u - 1)
                for r in range(UNIT):
                    at = HI * (r % 4)
                    for half in range(HALVES):
                        col = r * HALVES + half
                        mm = nc.tensor.matmul(ps[:, 2 * (u % 2) + r // 4, at:at + HI], lo[:, col, :], hi[:, col, :],
                                              start=(half == 0), stop=(half == HALVES - 1))
                mm.then_inc(counts_full, 1)

            def pool_slice(b, par, u, of, table_waits=False):
                if u == 0:
                    pe.wait_ge(counts_out, b * UNITS + UNITS)
                c = cnt(par)
                for hi in range(HI * u // of, HI * (u + 1) // of):
                    if table_waits and (hi % THI == 0 or hi == HI * u // of):
                        pe.wait_ge(low_done, hi // THI + 1)
                    mm = nc.tensor.matmul(ps[:, X_BANK + par, 0:3 * D], c[:, hi, :], parts(hi),
                                          start=(hi == 0), stop=(hi == HI - 1))
                if u == of - 1:
                    mm.then_inc(x_full, 1)

            def quad(j):
                return slice(CH * j, CH * j + CH)

            def x_part(place, seg, x, ks=(0, 1)):
                s, c0, n = seg
                for k in ks:
                    for j in range(NJ):
                        mm = nc.tensor.matmul(place(quad(j), s), x[:, CH * k:CH * k + CH],
                                              wih[:, k, j * 512 + c0:j * 512 + c0 + n],
                                              start=(k == 0), stop=(k == 1))
                return mm

            def h_part(r, place, seg, par, ks=range(KH)):
                s, c0, n = seg
                for k in ks:
                    for j in range(NJ):
                        mm = nc.tensor.matmul(place(quad(j), s), hT[par][:, CH * k:CH * k + CH],
                                              whh_v[:, k, j * 512 + c0:j * 512 + c0 + n],
                                              start=(k == 0 and not r.keep), stop=(k == KH - 1))
                if KH - 1 in ks:
                    mm.then_inc(r.full[s], 1)

            def turn_h(r, s):
                pe.wait_ge(r.h, s + 1)
                nc.tensor.transpose(hT_ps, h_now, ident[:, :]).then_inc(r.turned, 1)

            def turn_x(b, par):
                pe.wait_ge(x_summed, b + 1)
                nc.tensor.transpose(xT_ps(par), xparts[:, par, 0:D], ident[:, :]).then_inc(xT_full, 1)

            def gx_gif(par, x, ks):
                mm = x_part(early(par), GIF, x, ks)
                if 1 in ks:
                    mm.then_inc(gx_full, 1)

            def gx_o(par, x):
                x_part(early(par), OUTG, x).then_inc(gx_full, 1)

            def x_of(par, half):
                return xT_new[:, par, half * 2 * CH:(half + 1) * 2 * CH]

            def beside(u, b, par, steps):
                v, half = u % HALF, u // HALF
                s, place = 2 * b + half, early(1 - par)
                if steps:
                    if v == 0:
                        pe.wait_ge(gx_copied, 2 * s + 1)
                        pe.wait_ge(warm.hT, s + 1)
                        h_part(warm, place, GIF, half, (0, 1))
                    if v in (1, 2):
                        h_part(warm, place, GIF, half, (v + 1,))
                if v == 3:
                    if half == 0:
                        pe.wait_ge(x_out, b + 2)
                    elif not steps:
                        pe.wait_ge(gx_copied, 2 * s)
                    gx_o(1 - par, x_of(par, half))
                if v == 4 and steps:
                    pe.wait_ge(gx_copied, 2 * s + 2)
                    h_part(warm, place, OUTG, half)
                if v == 5:
                    if steps:
                        pe.wait_ge(warm.gif, s + 1)
                    else:
                        pe.wait_ge(gx_copied, 2 * s + 1)
                    if half == 1:
                        pe.wait_ge(xT_out, b + 2)
                    gx_gif(1 - par, x_of(half ^ par, 1 - half), (0,))
                if v == 6:
                    gx_gif(1 - par, x_of(half ^ par, 1 - half), (1,))

            def body(b, par, table_waits=False, pool=True, turn=True, x=True, steps=True):
                for u in range(UNITS):
                    histogram(b, u, first_block=not pool)
                    if x and steps and u % HALF == HALF - 1:
                        turn_h(warm, 2 * (b - 3) + u // HALF)
                    if pool:
                        pool_slice(b - 1, 1 - par, u, UNITS, table_waits)
                    if x:
                        beside(u, b - 3, 1 - par, steps)
                    if turn and u == 2:
                        if not steps and b == WARM_END:
                            pe.wait_ge(seam1_set, 1)
                        turn_x(b - 2, par)

            body(0, 0, pool=False, turn=False, x=False)
            body(1, 1, table_waits=True, turn=False, x=False)
            body(2, 0, x=False)
            pe.wait_ge(wih_in, 16)
            pe.wait_ge(xT_out, 1)
            gx_gif(1, x_of(0, 0), (0, 1))
            pe.wait_ge(whh_in, 16)
            with pe.Fori(0, WARM_BLOCKS // 2) as i:
                for e in range(2):
                    body(2 * i + e + 3, 1 - e)

            def seam(done):
                nc.tensor.matmul(seam_ps[:, 0:P], shift[:, :], c_now, start=True, stop=True)
                nc.tensor.matmul(seam_ps[:, P:2 * P], h_now, shift[:, :], start=True, stop=True).then_inc(done, 1)

            pe.wait_ge(warm.hT, WARM + 1)
            pe.wait_ge(shift_set, 1)
            seam(seam1)
            for b in range(WARM_BLOCKS + 3, BLOCKS):
                body(b, b % 2, steps=False)

            def gx(s, seg):
                par = s // 2 % 2
                pe.wait_ge(gx_copied, 2 * s - 1 if seg is GIF else 2 * s)
                if seg is GIF:
                    gx_gif(par, x_of(par, s % 2), (0, 1))
                else:
                    gx_o(1 - par, x_of(par, s % 2))

            s = 2 * (BLOCKS - 3)
            pool_slice(BLOCKS - 1, 1, 0, 2)
            turn_x(BLOCKS - 2, 0)
            pe.wait_ge(x_out, BLOCKS - 1)
            gx(s, OUTG)
            gx(s + 1, GIF)
            gx(s + 1, OUTG)
            pool_slice(BLOCKS - 1, 1, 1, 2)
            pe.wait_ge(xT_out, BLOCKS - 1)
            gx(s + 2, GIF)
            pe.wait_ge(x_out, BLOCKS)
            gx(s + 2, OUTG)
            gx(s + 3, GIF)
            turn_x(BLOCKS - 1, 1)
            gx(s + 3, OUTG)
            pe.wait_ge(xT_out, BLOCKS)
            for t in (s + 4, s + 5):
                gx(t, GIF)
                gx(t, OUTG)

            def gx_part(r, place, m, loads):
                pe.wait_ge(r.x_in[m], loads)
                for g, c0, n in (GIF, OUTG):
                    nc.tensor.matmul(place(EVERY, g), ident[:, :], gx_old[:, m, c0:c0 + n], start=True, stop=False)

            def hidden(r, l, m, ks):
                for k in ks:
                    mm = nc.tensor.matmul(h1_ps[:, m, :].rearrange("p (l c) -> p l c", c=CH),
                                          w1_sb[:, k, m * P:(m + 1) * P],
                                          hs[:, bass.ds(l, GROUP), CH * k:CH * k + CH],
                                          start=(k == 0), stop=(k == KH - 1))
                if KH - 1 in ks:
                    mm.then_inc(r.h1_full, 1)

            def outputs(r, g):
                pe.wait_ge(r.h1, 2 * g + 2)
                nc.tensor.matmul(y_ps, ones[0:1, :], bo_sb[0:1, :], start=True, stop=False)
                for m in range(2):
                    mm = nc.tensor.matmul(y_ps, h1[:, m, :], wo_sb[:, m, :], start=False, stop=(m == 1))
                mm.then_inc(r.y_full, 1)

            def group(r, base, i, turns, head=True):
                for q in range(GROUP):
                    s = GROUP * (base + i) + q
                    par = q % 2
                    if head or q > 0:
                        pe.wait_ge(r.hT, s)
                    h_part(r, later(par), GIF, par)
                    h_part(r, later(par), OUTG, par)
                    if not (i is LAST and q == GROUP - 1):
                        gx_part(r, later(1 - par), (q + 1) % GROUP, turns + 16 * i + (32 if q == GROUP - 1 else 16))
                    if head:
                        if q == 0:
                            pe.wait_ge(r.kept, s + 2)
                        if q < 2:
                            hidden(r, GROUP * (i - 1), q, (0,))
                        if q == 3:
                            outputs(r, base + i - 1)
                    turn_h(r, s)
                    if head and q < 2:
                        hidden(r, GROUP * (i - 1), q, (1, 2, 3))

            def run(r, base, turns, begin):
                gx_part(r, later(0), 0, turns + 16)
                begin()
                group(r, base, 0, turns, head=False)
                pe.wait_ge(head_in, 64)
                with pe.Fori(1, LAST) as i:
                    group(r, base, i, turns)
                group(r, base, LAST, turns)

            def last_outputs(r, base):
                pe.wait_ge(r.kept, GROUP * (base + GROUPS) + 2)
                for m in range(2):
                    hidden(r, L - GROUP, m, range(KH))
                pe.wait_ge(r.y_out, base + LAST)
                outputs(r, base + LAST)

            run(main, 0, 0, lambda: pe.wait_ge(seam1_set, 1))

            def vote(r, n):
                pe.wait_ge(r.hT, L)
                seam(seam2)
                last_outputs(r, 0)
                pe.wait_ge(compare, n + 1)
                pe.wait_ge(r.y_out, GROUPS)
                nc.tensor.matmul(votes_ps, agree_row, ones[:, 0:1], start=True, stop=True)\
                    .then_inc(agree_sum, 1)

            vote(main, 0)
            with redo_needed(pe, 0):
                pe.wait_ge(restarted, 1)
                run(again, 0, 0, lambda: None)
                vote(again, 1)
                with redo_needed(pe, 1):
                    with pe.Fori(1, CH - 1) as n:
                        seam(seam2)
                        pe.wait_ge(restarted, n + 1)
                        run(again, n * GROUPS, n * 4 * L, lambda: None)
                        last_outputs(again, n * GROUPS)
                pe.nop()

        @block.scalar
        def _(act):
            def split(part_n, k):
                if part_n == 0:
                    act.wait_ge(table_in[k], 32 if k == TCHUNKS - 1 else 16)
                else:
                    act.wait_ge((rest1_done, rest2_done)[part_n - 1], k + 1)
                nc.scalar.activation(tpart(part_n, k), stage_v(k), ACT.Copy)\
                    .then_inc((top_done, mid_done, low_done)[part_n], 1)

            def take_counts(b, par, g):
                act.wait_ge(counts_full, b * UNITS + g + 1)
                at = ps[:, 2 * (g % 2):2 * (g % 2) + 2, 0:4 * HI].rearrange("p b (r h) -> p h b r", h=HI)
                nc.scalar.activation(cnt(par)[:, :, g * UNIT:(g + 1) * UNIT].rearrange("p h (b r) -> p h b r", b=2),
                                     at, ACT.Copy).then_inc(counts_out, 1)

            def x_rows_out(b, par):
                act.wait_ge(x_full, b + 1)
                nc.scalar.activation(xparts[:, par, :], ps[:, X_BANK + par, 0:3 * D], ACT.Copy,
                                     scale=1.0 / MEAN_OVER).then_inc(x_out, 1)

            def x_turned_out(b, par):
                act.wait_ge(xT_full, b + 1)
                nc.scalar.activation(xT_new[:, par, :], xT_ps(par), ACT.Copy).then_inc(xT_out, 1)

            def gx_gif_out(s, buf, par, kept):
                if kept is not None:
                    act.wait_ge(gx_kept[buf], kept)
                act.wait_ge(gx_full, 2 * s + 1)
                nc.scalar.activation(gx_new[:, buf, 0:3 * P], early(par)(EVERY, 0), ACT.Copy).then_inc(gx_copied, 1)

            def gx_o_out(s, buf, par):
                act.wait_ge(gx_full, 2 * s + 2)
                nc.scalar.activation(gx_new[:, buf, 3 * P:4 * P], early(par)(EVERY, 1), ACT.Copy).then_inc(gx_copied, 1)

            def act_gif(r, s, place):
                act.wait_ge(r.gates[0], s + 1)
                nc.scalar.activation(sig_if, place(EVERY, 0)[:, P:3 * P], ACT.Sigmoid)
                nc.scalar.activation(tanh_g, place(EVERY, 0)[:, 0:P], ACT.Tanh).then_inc(r.gif, 1)

            def act_o(r, s, place):
                act.wait_ge(r.gates[1], s + 1)
                nc.scalar.activation(sig_o, place(EVERY, 1), ACT.Sigmoid).then_inc(r.o, 1)

            def act_c(r, s):
                act.wait_ge(r.c, s + 1)
                nc.scalar.activation(tanh_c, c_now, ACT.Tanh).then_inc(r.tc, 1)

            def body(b, par, turn=True, x=True, steps=True, splits=None):
                if turn:
                    x_rows_out(b - 2, par)
                for u in range(UNITS):
                    take_counts(b, par, u)
                    if splits is not None:
                        splits(b * UNITS + u)
                    if turn and u == 3:
                        x_turned_out(b - 2, par)
                    if x:
                        v, half = u % HALF, u // HALF
                        s = 2 * (b - 3) + half
                        if v == 3:
                            if steps:
                                act_gif(warm, s, early(par))
                            gx_o_out(s, half, par)
                        if steps and v == 4:
                            act_c(warm, s)
                        if steps and v == 5:
                            act_o(warm, s, early(par))
                        if v == 6:
                            first = half == 0 and b is FIRST_STEPS
                            gx_gif_out(s + 1, 1 - half, par, None if first else 16 * (b - 3 + half))
                        if v == 7:
                            if steps:
                                act.wait_ge(warm.turned, s + 1)
                                nc.scalar.activation(hT[1 - half], hT_ps, ACT.Copy).then_inc(warm.hT, 1)

            act.wait_ge(ones_set, 1)
            nc.scalar.activation(xparts[:, 0, 0:1], ones[:, 0:1], ACT.Sigmoid)
            nc.scalar.activation(hT[0], ones[:, :], ACT.Copy, scale=0.0).then_inc(warm.hT, 1)

            def splits(unit):
                for k in range(TCHUNKS):
                    for part_n in range(3):
                        if unit == SPLIT_AT[part_n][k]:
                            split(part_n, k)

            split(0, 0)
            body(0, 0, turn=False, x=False, splits=splits)
            act.wait_ge(low_done, TCHUNKS - STAGED)
            body(1, 1, turn=False, x=False, splits=splits)
            body(2, 0, x=False)
            gx_gif_out(0, 0, 1, None)
            body(FIRST_STEPS, 1)
            with act.Fori(0, WARM_BLOCKS // 2 - 1) as i:
                for e in range(2):
                    body(2 * i + e + 4, e)
            body(WARM_BLOCKS + 2, 0)
            for b in range(WARM_BLOCKS + 3, BLOCKS):
                body(b, b % 2, steps=False)

            def gx_out_of(s, seg):
                if seg is GIF:
                    gx_gif_out(s, s % 2, 0, 16 * (s // 2))
                else:
                    gx_o_out(s, s % 2, 1 - s // 2 % 2)

            s = 2 * (BLOCKS - 3)
            x_rows_out(BLOCKS - 2, 0)
            x_turned_out(BLOCKS - 2, 0)
            for t, seg in ((s, OUTG), (s + 1, GIF), (s + 1, OUTG)):
                gx_out_of(t, seg)
            x_rows_out(BLOCKS - 1, 1)
            for t, seg in ((s + 2, GIF), (s + 2, OUTG), (s + 3, GIF)):
                gx_out_of(t, seg)
            x_turned_out(BLOCKS - 1, 1)
            for t, seg in ((s + 3, OUTG), (s + 4, GIF), (s + 4, OUTG), (s + 5, GIF), (s + 5, OUTG)):
                gx_out_of(t, seg)

            def rectify(r, g, m):
                act.wait_ge(r.h1_full, 2 * g + m + 1)
                nc.scalar.activation(h1[:, m, :], h1_ps[:, m, :], ACT.Relu, bias=b1_sb[:, m:m + 1]).then_inc(r.h1, 1)

            def group(r, base, i, head=True):
                for q in range(GROUP):
                    s = GROUP * (base + i) + q
                    act_gif(r, s, later(q % 2))
                    act_o(r, s, later(q % 2))
                    act_c(r, s)
                    if head and q in (1, 2):
                        rectify(r, base + i - 1, q - 1)

            def run(r, base):
                group(r, base, 0, head=False)
                act.wait_ge(head_in, 64)
                with act.Fori(1, GROUPS) as i:
                    group(r, base, i)
                for m in range(2):
                    rectify(r, base + LAST, m)

            run(main, 0)
            with redo_needed(act, 0):
                run(again, 0)
                with redo_needed(act, 1):
                    with act.Fori(1, CH - 1) as n:
                        run(again, n * GROUPS)
                act.nop()

        @block.vector
        def _(dve):
            dve.wait_ge(ramp_ready, 1)
            nc.vector.tensor_copy(ramp[:, :], ramp32).then_inc(ramp_ready, 1)
            dve.wait_ge(ramp_ready, 2)

            def decode(b, buf):
                dve.wait_ge(raw_in[buf], 16 * b + 16)
                low16 = raw[:, buf, :].bitcast(I16).rearrange("p (c e) -> p c e", e=2)[:, :, 0:1]\
                    .to_broadcast([P, BLOCK * HALVES, 2])
                nc.vector.tensor_scalar(lo2[:, :, :], low16, LO - 1, None, ALU.bitwise_and).then_inc(decoded, 1)
                nc.vector.tensor_scalar(hi2[:, :, :], low16, 7, None, ALU.logical_shift_right).then_inc(decoded, 1)

            def one_hot(codes_v, n, pairs, u):
                c = pairs[:, UC * u:UC * u + UC, :].unsqueeze(2).to_broadcast([P, UC, n // 2, 2])
                r = ramp[:, 0:n].rearrange("p (v e) -> p v e", e=2).unsqueeze(1).to_broadcast([P, UC, n // 2, 2])
                return nc.vector.tensor_tensor(codes_v.rearrange("p c (v e) -> p c v e", e=2), c, r, ALU.is_equal)

            def add_gx(r, s, par, buf, seg):
                g, c0, n = seg
                dve.wait_ge(gx_out, 2 * s + 1 + g)
                dve.wait_ge(r.full[g], s + 1)
                at = early(par)(EVERY, g)
                nc.vector.tensor_tensor(at, at, gx_new[:, buf, c0:c0 + n], ALU.add).then_inc(r.gates[g], 1)

            def dve_c(r, s):
                dve.wait_ge(r.gif, s + 1)
                nc.vector.tensor_tensor(products, sig_if, gc, ALU.mult).then_inc(r.terms, 1)
                dve.wait_ge(r.terms, s + 1)
                nc.vector.tensor_tensor(c_now, products[:, 0:P], products[:, P:2 * P], ALU.add).then_inc(r.c, 1)

            def dve_h(r, s):
                dve.wait_ge(r.o, s + 1)
                dve.wait_ge(r.tc, s + 1)
                nc.vector.tensor_tensor(h_now, sig_o, tanh_c, ALU.mult).then_inc(r.h, 1)

            def dve_hT(r, s, par):
                if r.keep:
                    dve.wait_ge(r.kept, s + 1)
                dve.wait_ge(r.turned, s + 1)
                nc.vector.tensor_copy(hT[1 - par], hT_ps).then_inc(r.hT, 1)

            def from_seam(done):
                nc.vector.tensor_copy(c_now, seam_ps[:, 0:P])
                nc.vector.tensor_copy(hT[0], seam_ps[:, P:2 * P]).then_inc(done, 1)

            def body(b, buf, turn, steps=True, first=False):
                if not first:
                    dve.wait_ge(codes_ready, b * UNITS)
                decode(turn, buf)
                dve.wait_ge(decoded, 2 * b + 2)
                for u in range(UNITS):
                    if not (first and u < 2):
                        dve.wait_ge(counts_full, b * UNITS + u - 1)
                    one_hot(lo_codes(u % 2), LO, lo2, u)
                    one_hot(hi_codes(u % 2), HI, hi2, u).then_inc(codes_ready, 1)
                    if not steps and u == 1 and b == WARM_END:
                        dve.wait_ge(seam1, 1)
                        from_seam(seam1_set)
                    if steps:
                        s = 2 * (b - 3) + u // HALF
                        if u % HALF == 4:
                            add_gx(warm, s, buf, u // HALF, GIF)
                        if u % HALF == 5:
                            dve_c(warm, s)
                        if u % HALF == 6:
                            add_gx(warm, s, buf, u // HALF, OUTG)
                        if u % HALF == 7:
                            dve_h(warm, s)

            nc.vector.memset(c_now, 0.0).then_inc(warm_c_zero, 1)
            body(0, 0, 0, steps=False, first=True)
            body(1, 1, 0, steps=False)
            body(2, 0, 1, steps=False)
            dve.wait_ge(warm_c_zero, 1)
            with dve.Fori(0, WARM_BLOCKS // 2) as i:
                for e in range(2):
                    body(2 * i + e + 3, 1 - e, i + 1 + e)

            for b in range(WARM_BLOCKS + 3, BLOCKS):
                body(b, b % 2, b // 2, steps=False)

            def outputs_out(r, g, stored):
                dve.wait_ge(r.y_full, g + 1)
                if stored:
                    dve.wait_ge(r.stored, 16 * g)
                nc.vector.tensor_copy(y_sb, y_ps).then_inc(r.y_out, 1)

            def group(r, base, i, head=True, stored=True):
                for q in range(GROUP):
                    s = GROUP * (base + i) + q
                    dve_c(r, s)
                    dve_h(r, s)
                    dve_hT(r, s, q % 2)
                if head:
                    outputs_out(r, base + i - 1, stored)

            def run(r, base, stored=False):
                group(r, base, 0, head=False)
                group(r, base, 1, stored=stored)
                with dve.Fori(2, GROUPS) as i:
                    group(r, base, i)

            def keep_start(done, n):
                dve.wait_ge(done, n)
                nc.vector.tensor_copy(start[:, 0:P], c_now)
                nc.vector.tensor_copy(start[:, P:2 * P], hT[0]).then_inc(start_kept, 1)
                dve.wait_ge(start_kept, n)

            def vote(r, n):
                dve.wait_ge(seam2, n + 1)
                nc.vector.tensor_tensor(diff, seam_ps, start, ALU.subtract).then_inc(compare_step, 1)
                dve.wait_ge(compare_step, 3 * n + 1)
                nc.vector.tensor_tensor(sq, diff, diff, ALU.mult).then_inc(compare_step, 1)
                dve.wait_ge(compare_step, 3 * n + 2)
                nc.vector.tensor_scalar(agree, sq, TOL * TOL, None, ALU.is_le).then_inc(compare_step, 1)
                dve.wait_ge(compare_step, 3 * n + 3)
                nc.vector.tensor_reduce(agree_row, agree, AX.X, ALU.add).then_inc(compare, 1)
                outputs_out(r, LAST, True)
                dve.wait_ge(agree_sum, n + 1)
                nc.vector.tensor_scalar(redo[0:1, :], votes_ps, float(2 * P * P), None, ALU.is_lt)\
                    .then_inc(redo_set, 1)

            dve.wait_ge(x_full, BLOCKS)
            keep_start(seam1_set, 1)
            run(main, 0)
            vote(main, 0)
            with redo_needed(dve, 0):
                dve.wait_ge(main.kept, L + 2)
                from_seam(restarted)
                keep_start(restarted, 1)
                run(again, 0)
                vote(again, 1)
                with redo_needed(dve, 1):
                    with dve.Fori(1, CH - 1) as n:
                        dve.wait_ge(again.kept, n * L + 2)
                        dve.wait_ge(seam2, n + 2)
                        from_seam(restarted)
                        run(again, n * GROUPS, stored=True)
                        outputs_out(again, n * GROUPS + LAST, True)
                dve.nop()

        @block.gpsimd
        def _(pool):
            nc.gpsimd.iota(ramp32, pattern=[[1, LO]], base=0, channel_multiplier=0).then_inc(ramp_ready, 1)
            nc.gpsimd.memset(stage(TCHUNKS - 1)[:, (THI - 1) * D:THI * D], 0.0).then_inc(tail_zero, 1)
            nc.gpsimd.memset(ident[:, :], 0.0).then_inc(blank, 1)
            nc.gpsimd.memset(shift[:, :], 0.0).then_inc(blank, 1)
            nc.gpsimd.memset(ones[:, :], 1.0).then_inc(ones_set, 1)
            pool.wait_ge(blank, 2)
            nc.gpsimd.affine_select(out=ident[:, :], in_=ident[:, :], compare_op=ALU.not_equal, fill=1.0,
                                    base=0, pattern=[[-1, P]], channel_multiplier=1).then_inc(ident_set, 1)
            nc.gpsimd.affine_select(out=shift[:, :], in_=shift[:, :], compare_op=ALU.not_equal, fill=1.0,
                                    base=1, pattern=[[-1, P]], channel_multiplier=1).then_inc(blank, 1)
            pool.wait_ge(blank, 3)
            nc.gpsimd.memset(shift[:, :].rearrange("p (j c) -> p j c", c=CH)[:, :, 0:1], 0.0).then_inc(shift_set, 1)

            def rest(n, k, wait, done):
                pool.wait_ge(wait, k + 1)
                nc.gpsimd.tensor_tensor(stage_v(k), stage_v(k), tpart(n, k), ALU.subtract).then_inc(done, 1)

            for step in range(TCHUNKS + 1):
                if step < TCHUNKS:
                    rest(0, step, top_done, rest1_done)
                if step >= 1:
                    rest(1, step - 1, mid_done, rest2_done)

            def sum_parts(b, par):
                pool.wait_ge(x_out, b + 1)
                top, mid, low = (xparts[:, par, n * D:(n + 1) * D] for n in range(3))
                nc.gpsimd.tensor_tensor(mid, mid, low, ALU.add).then_inc(x_half, 1)
                pool.wait_ge(x_half, b + 1)
                nc.gpsimd.tensor_tensor(top, top, mid, ALU.add).then_inc(x_summed, 1)

            def gx_piece(s, buf, seg):
                g, c0, n = seg
                at = gx_new[:, buf, c0:c0 + n]
                pool.wait_ge(gx_copied, 2 * s + 1 + g)
                nc.gpsimd.tensor_tensor(at, at, bias[:, c0:c0 + n], ALU.add).then_inc(gx_out, 1)

            def beside(b, par):
                sum_parts(b - 2, par)
                for half in range(2):
                    s = 2 * (b - 3) + half
                    gx_piece(s, half, OUTG)
                    gx_piece(s + 1, 1 - half, GIF)

            pool.wait_ge(bias_in, 16 * 2 * NJ)
            nc.gpsimd.tensor_tensor(bias[:, :], bias[:, :], gx_new[:, 0, :], ALU.add).then_inc(bias_ready, 1)
            pool.wait_ge(bias_ready, 1)
            sum_parts(0, 0)
            gx_piece(0, 0, GIF)
            beside(FIRST_STEPS, 1)
            with pool.Fori(0, (BLOCKS - FIRST_STEPS - 1) // 2) as i:
                for e in range(2):
                    beside(2 * i + e + FIRST_STEPS + 1, e)

            s = 2 * (BLOCKS - 3)
            sum_parts(BLOCKS - 2, 0)
            gx_piece(s, s % 2, OUTG)
            gx_piece(s + 1, (s + 1) % 2, GIF)
            gx_piece(s + 1, (s + 1) % 2, OUTG)
            sum_parts(BLOCKS - 1, 1)
            for t in range(s + 2, s + 6):
                gx_piece(t, t % 2, GIF)
                gx_piece(t, t % 2, OUTG)

            def run(r, base):
                with pool.Fori(0, L // 2) as i:
                    for par in range(2):
                        pool.wait_ge(r.hT, base + 2 * i + par + 1)
                        nc.gpsimd.tensor_copy(hs[:, bass.ds(2 * i + par, 1), :], hT[1 - par].unsqueeze(1))\
                            .then_inc(r.kept, 1)

            pool.sem_inc(main.kept, 2)
            run(main, 0)
            with redo_needed(pool, 0):
                pool.sem_inc(again.kept, 2)
                run(again, 0)
                with redo_needed(pool, 1):
                    with pool.Fori(1, CH - 1) as n:
                        run(again, n * L)
                pool.nop()


def kernel(r_diag_idx, r_proc_idx, L0_rec_embedding, L0_rec_W_ih, L0_rec_W_hh, L0_rec_b_ih, L0_rec_b_hh,
           L0_rec_W1, L0_rec_b1, L0_rec_W_out, L0_rec_b_out):
    import numpy as np
    import concourse.bacc as bacc
    from concourse.bass_utils import run_bass_kernel_spmd

    def a(x):
        return np.asarray(x)

    idx = np.stack([a(r_diag_idx), a(r_proc_idx)]).reshape(2, CH, BLOCKS, 2, HALVES, P)
    idx = np.roll(idx.transpose(2, 5, 3, 0, 1, 4), -(FIRST // 2), axis=0)
    order = [2, 0, 1, 3]

    def gates(w):
        return w.reshape(4, NJ, P, -1)[order].transpose(1, 0, 2, 3).reshape(G4, -1)

    def tall(w):
        n = w.shape[0]
        return w.reshape(n, -1, P).transpose(2, 1, 0).reshape(P, -1)

    arrays = {
        "raw_idx": idx.reshape(BLOCKS, P, BLOCK * HALVES),
        "table": a(L0_rec_embedding),
        "w_ih": tall(gates(a(L0_rec_W_ih))),
        "w_hh": tall(gates(a(L0_rec_W_hh))),
        "b_ih": gates(a(L0_rec_b_ih)).reshape(1, G4),
        "b_hh": gates(a(L0_rec_b_hh)).reshape(1, G4),
        "w1": tall(a(L0_rec_W1)),
        "b1": a(L0_rec_b1).reshape(2, P).T,
        "w_out": tall(a(L0_rec_W_out)),
        "b_out": a(L0_rec_b_out).reshape(1, C),
    }
    arrays = {name: np.ascontiguousarray(x) for name, x in arrays.items()}
    nc = bacc.Bacc("TRN2", target_bir_lowering=False, num_devices=1)
    args = [nc.dram_tensor(name, x.shape, mybir.dt.from_np(x.dtype), kind="ExternalInput").ap()
            for name, x in arrays.items()]
    out = nc.dram_tensor("out", (T, C), F32, kind="ExternalOutput").ap()
    lstm_kernel(nc, *args, out)
    got = run_bass_kernel_spmd(nc, [arrays], core_ids=[0])
    return got.results[0]["out"]
```
